# Optimizing a Trainium2 kernel written in Bass

```python
import numpy as np
import jax
import jax.numpy as jnp

def _softmax(x, axis=-1):
    return jax.nn.softmax(x, axis=axis)

def _gelu(x):
    return jax.nn.gelu(x, approximate=True)

def _silu(x):
    return jax.nn.silu(x)

def _sigmoid(x):
    return jax.nn.sigmoid(x)

def _layernorm(x, axis=-1, eps=1e-05):
    m = jnp.mean(x, axis=axis, keepdims=True)
    v = jnp.var(x, axis=axis, keepdims=True)
    return (x - m) / jnp.sqrt(v + eps)

def _scatter_add(tgt, idx, src, axis=0):
    return tgt.at[idx].add(src)

def _segment_sum(src, seg, n):
    return jax.ops.segment_sum(src, seg, n)
kernel_name = 'mk_dlrm_tower_d1_rec_r8_531f4c'

def setup_inputs(seed: int=0):
    np.random.seed(seed)
    _w = jnp.asarray

    def _rec_inputs():
        import jax
        import jax.numpy as jnp
        _tk = jax.random.key(seed)
        ids = jnp.stack([jax.random.randint(jax.random.fold_in(_tk, 200 + f), (2048,), 0, v, jnp.int32) for f, v in enumerate([12500, 1000, 1000, 12500, 1000, 1250, 125000, 1000, 1000, 1250, 1000, 12500, 1000, 12500, 1000, 1000, 1000, 12500, 1000, 1000, 1250, 1000, 1000, 1000, 1000, 12500])], axis=1)
        tbl_0 = 0.05 * jax.random.normal(jax.random.fold_in(_tk, 500 + 0), (12500, 128), jnp.float32)
        tbl_1 = 0.05 * jax.random.normal(jax.random.fold_in(_tk, 500 + 1), (1000, 128), jnp.float32)
        tbl_2 = 0.05 * jax.random.normal(jax.random.fold_in(_tk, 500 + 2), (1000, 128), jnp.float32)
        tbl_3 = 0.05 * jax.random.normal(jax.random.fold_in(_tk, 500 + 3), (12500, 128), jnp.float32)
        tbl_4 = 0.05 * jax.random.normal(jax.random.fold_in(_tk, 500 + 4), (1000, 128), jnp.float32)
        tbl_5 = 0.05 * jax.random.normal(jax.random.fold_in(_tk, 500 + 5), (1250, 128), jnp.float32)
        tbl_6 = 0.05 * jax.random.normal(jax.random.fold_in(_tk, 500 + 6), (125000, 128), jnp.float32)
        tbl_7 = 0.05 * jax.random.normal(jax.random.fold_in(_tk, 500 + 7), (1000, 128), jnp.float32)
        tbl_8 = 0.05 * jax.random.normal(jax.random.fold_in(_tk, 500 + 8), (1000, 128), jnp.float32)
        tbl_9 = 0.05 * jax.random.normal(jax.random.fold_in(_tk, 500 + 9), (1250, 128), jnp.float32)
        tbl_10 = 0.05 * jax.random.normal(jax.random.fold_in(_tk, 500 + 10), (1000, 128), jnp.float32)
        tbl_11 = 0.05 * jax.random.normal(jax.random.fold_in(_tk, 500 + 11), (12500, 128), jnp.float32)
        tbl_12 = 0.05 * jax.random.normal(jax.random.fold_in(_tk, 500 + 12), (1000, 128), jnp.float32)
        tbl_13 = 0.05 * jax.random.normal(jax.random.fold_in(_tk, 500 + 13), (12500, 128), jnp.float32)
        tbl_14 = 0.05 * jax.random.normal(jax.random.fold_in(_tk, 500 + 14), (1000, 128), jnp.float32)
        tbl_15 = 0.05 * jax.random.normal(jax.random.fold_in(_tk, 500 + 15), (1000, 128), jnp.float32)
        tbl_16 = 0.05 * jax.random.normal(jax.random.fold_in(_tk, 500 + 16), (1000, 128), jnp.float32)
        tbl_17 = 0.05 * jax.random.normal(jax.random.fold_in(_tk, 500 + 17), (12500, 128), jnp.float32)
        tbl_18 = 0.05 * jax.random.normal(jax.random.fold_in(_tk, 500 + 18), (1000, 128), jnp.float32)
        tbl_19 = 0.05 * jax.random.normal(jax.random.fold_in(_tk, 500 + 19), (1000, 128), jnp.float32)
        tbl_20 = 0.05 * jax.random.normal(jax.random.fold_in(_tk, 500 + 20), (1250, 128), jnp.float32)
        tbl_21 = 0.05 * jax.random.normal(jax.random.fold_in(_tk, 500 + 21), (1000, 128), jnp.float32)
        tbl_22 = 0.05 * jax.random.normal(jax.random.fold_in(_tk, 500 + 22), (1000, 128), jnp.float32)
        tbl_23 = 0.05 * jax.random.normal(jax.random.fold_in(_tk, 500 + 23), (1000, 128), jnp.float32)
        tbl_24 = 0.05 * jax.random.normal(jax.random.fold_in(_tk, 500 + 24), (1000, 128), jnp.float32)
        tbl_25 = 0.05 * jax.random.normal(jax.random.fold_in(_tk, 500 + 25), (12500, 128), jnp.float32)
        _rk = jax.random.fold_in(_tk, 7)
        r_dense = -0.000520686 + 1.00062 * jax.random.normal(jax.random.fold_in(_rk, 101), (2048, 128), jnp.float32)
        W_top1 = 0.0456912 * jax.random.normal(jax.random.fold_in(_tk, 801), (479, 512), jnp.float32)
        W_top2 = 0.0441942 * jax.random.normal(jax.random.fold_in(_tk, 802), (512, 256), jnp.float32)
        W_top3 = 0.0625 * jax.random.normal(jax.random.fold_in(_tk, 803), (256, 1), jnp.float32)
        b_top1 = jnp.zeros((512,), jnp.float32)
        b_top2 = jnp.zeros((256,), jnp.float32)
        return (r_dense, ids, tbl_0, tbl_1, tbl_2, tbl_3, tbl_4, tbl_5, tbl_6, tbl_7, tbl_8, tbl_9, tbl_10, tbl_11, tbl_12, tbl_13, tbl_14, tbl_15, tbl_16, tbl_17, tbl_18, tbl_19, tbl_20, tbl_21, tbl_22, tbl_23, tbl_24, tbl_25, W_top1, b_top1, W_top2, b_top2, W_top3)
    r_dense, ids, tbl_0, tbl_1, tbl_2, tbl_3, tbl_4, tbl_5, tbl_6, tbl_7, tbl_8, tbl_9, tbl_10, tbl_11, tbl_12, tbl_13, tbl_14, tbl_15, tbl_16, tbl_17, tbl_18, tbl_19, tbl_20, tbl_21, tbl_22, tbl_23, tbl_24, tbl_25, W_top1, b_top1, W_top2, b_top2, W_top3 = _rec_inputs()

    def _L0_rec_setup():
        import jax, jax.numpy as jnp
        import numpy as np
        B, NUM_EMBS, D = (2048, 26, 128)
        key = jax.random.key(seed)
        k1, k2 = jax.random.split(key)
        dense = jax.random.normal(k1, (B, D), dtype=jnp.float32)
        embs = jax.random.normal(k2, (B, NUM_EMBS, D), dtype=jnp.float32)
        return {'dense': dense, 'embs': embs}
    _L0_rec_all = _L0_rec_setup()
    _L0_rec_in = {k: v for k, v in _L0_rec_all.items() if k in ()}
    del _L0_rec_all
    return {'r_dense': r_dense, 'ids': ids, 'tbl_0': tbl_0, 'tbl_1': tbl_1, 'tbl_2': tbl_2, 'tbl_3': tbl_3, 'tbl_4': tbl_4, 'tbl_5': tbl_5, 'tbl_6': tbl_6, 'tbl_7': tbl_7, 'tbl_8': tbl_8, 'tbl_9': tbl_9, 'tbl_10': tbl_10, 'tbl_11': tbl_11, 'tbl_12': tbl_12, 'tbl_13': tbl_13, 'tbl_14': tbl_14, 'tbl_15': tbl_15, 'tbl_16': tbl_16, 'tbl_17': tbl_17, 'tbl_18': tbl_18, 'tbl_19': tbl_19, 'tbl_20': tbl_20, 'tbl_21': tbl_21, 'tbl_22': tbl_22, 'tbl_23': tbl_23, 'tbl_24': tbl_24, 'tbl_25': tbl_25, 'W_top1': W_top1, 'b_top1': b_top1, 'W_top2': W_top2, 'b_top2': b_top2, 'W_top3': W_top3}

def reference(r_dense, ids, tbl_0, tbl_1, tbl_2, tbl_3, tbl_4, tbl_5, tbl_6, tbl_7, tbl_8, tbl_9, tbl_10, tbl_11, tbl_12, tbl_13, tbl_14, tbl_15, tbl_16, tbl_17, tbl_18, tbl_19, tbl_20, tbl_21, tbl_22, tbl_23, tbl_24, tbl_25, W_top1, b_top1, W_top2, b_top2, W_top3):
    import jax
    import jax.numpy as jnp

    def _L0_rec_ref(dense, embs):
        import jax, jax.numpy as jnp
        import numpy as np
        B, NUM_EMBS, D = (2048, 26, 128)
        T = jnp.concatenate([dense[:, None, :], embs], axis=1)
        N = T.shape[1]
        Z = jnp.einsum('bnd,bmd->bnm', T, T)
        iu0, iu1 = jnp.triu_indices(N, k=1)
        return Z[:, iu0, iu1]
    e = jnp.stack([tbl_0[ids[:, 0]], tbl_1[ids[:, 1]], tbl_2[ids[:, 2]], tbl_3[ids[:, 3]], tbl_4[ids[:, 4]], tbl_5[ids[:, 5]], tbl_6[ids[:, 6]], tbl_7[ids[:, 7]], tbl_8[ids[:, 8]], tbl_9[ids[:, 9]], tbl_10[ids[:, 10]], tbl_11[ids[:, 11]], tbl_12[ids[:, 12]], tbl_13[ids[:, 13]], tbl_14[ids[:, 14]], tbl_15[ids[:, 15]], tbl_16[ids[:, 16]], tbl_17[ids[:, 17]], tbl_18[ids[:, 18]], tbl_19[ids[:, 19]], tbl_20[ids[:, 20]], tbl_21[ids[:, 21]], tbl_22[ids[:, 22]], tbl_23[ids[:, 23]], tbl_24[ids[:, 24]], tbl_25[ids[:, 25]]], axis=1)
    z = _L0_rec_ref(r_dense, e)
    z = z.reshape(z.shape[0], -1)
    h = jnp.concatenate([z, r_dense], axis=1)
    h = jnp.maximum(h @ W_top1 + b_top1, 0.0)
    h = jnp.maximum(h @ W_top2 + b_top2, 0.0)
    y = h @ W_top3
    return y

_drawn_inputs = setup_inputs


def setup_inputs(seed=0):
    import zlib

    import numpy as np

    out = dict(_drawn_inputs(seed))
    spreads = {'b_top1': (0.0, 0.1), 'b_top2': (0.0, 0.1)}
    factors = {}
    for name, (base, spread) in spreads.items():
        noise = np.random.default_rng([zlib.crc32(name.encode()), seed]).standard_normal(out[name].shape)
        drawn = base * np.exp(spread * noise) if base else spread * noise
        out[name] = jnp.asarray(drawn.astype(out[name].dtype))
    for name, factor in factors.items():
        out[name] = (out[name] * factor).astype(out[name].dtype)
    return out
```

```python
from contextlib import ExitStack

import concourse.bass as bass
from concourse import mybir

F32 = mybir.dt.float32
F32R = mybir.dt.float32r
I32 = mybir.dt.int32
ALU = mybir.AluOpType
ACT = mybir.ActivationFunctionType

P = 128
BATCH, FIELDS, D = 2048, 26, 128
H1, H2 = 512, 256

ONEHOT = (1, 2, 4, 7, 8, 10)
GATHERED = tuple(f for f in range(FIELDS) if f not in ONEHOT)
TABLE_ROWS = 1000
ROWS_PER_PART = 8
TABLE_PARTS = TABLE_ROWS // ROWS_PER_PART

VECTORS = (0,) + tuple(f + 1 for f in GATHERED) + tuple(f + 1 for f in ONEHOT)
NVEC = len(VECTORS)
SLOT = 32

TILE = 128
TILES = 2
STEP = TILE * TILES
STEPS = BATCH // STEP

PAIR_COLS = 7
PAIR_START = (0, 7, 14, NVEC - PAIR_COLS)
BLOCKS = len(PAIR_START)
CHUNKS = PAIR_COLS + 1


def bass_dlrm_tower(nc, dense, ids, ids_onehot, tables, w1, b1, w2, b2, w3, out):
    NG, NO = len(GATHERED), len(ONEHOT)
    KH1, KH2 = H1 // P, H2 // P

    PER_CHUNK = 4
    NT = NG + 1
    OH_CHUNKS = NO // 2
    T_CHUNKS = -(-NT // PER_CHUNK)
    VCHUNKS = OH_CHUNKS + TILES * T_CHUNKS
    V_ACT, V_DVE = (VCHUNKS + 1) // 2, VCHUNKS // 2

    GROUP = 4
    SET_BANKS, BANK_GROUPS = 2, 4
    SET = SET_BANKS * BANK_GROUPS * GROUP
    SETS = TILE // SET
    PRODUCTS = GROUP * NVEC

    HALF = ROWS_PER_PART // 2
    PIECES = 2 * NO
    RING = 3
    AHEAD = 3
    assert PIECES % RING == 0 and AHEAD <= RING

    def wait(engine, semaphore, value):
        if not (isinstance(value, int) and value <= 0):
            engine.wait_ge(semaphore, value)

    with ExitStack() as ctx:
        def sb(name, shape, dt):
            return ctx.enter_context(nc.sbuf_tensor(name, shape, dt))

        def psum(name, shape):
            return ctx.enter_context(nc.psum_tensor(name, shape, F32))

        def sem(name):
            return ctx.enter_context(nc.semaphore(name))

        ident = sb("ident", [P, P], F32)
        row_base = sb("row_base", [P, 1], I32)
        idx = [sb(f"idx{t}", [P, FIELDS], I32) for t in range(TILES)]
        ids_bc = sb("ids_bc", [P, NO, STEP], I32)
        row_off = sb("row_off", [P, NO, STEP], F32)
        onehot = sb("onehot", [P, RING, HALF, STEP], F32R)
        tab_hi = sb("tab_hi", [P, NO, ROWS_PER_PART, D], F32R)
        tab_lo = sb("tab_lo", [P, NO, ROWS_PER_PART, D], F32R)
        rows = [sb(f"rows{t}", [P, NG, D], F32) for t in range(TILES)]
        dense_in = [sb(f"dense_in{t}", [P, D], F32) for t in range(TILES)]
        vecs = sb("vecs", [P, TILES, TILE, SLOT], F32)
        feat = sb("feat", [P, CHUNKS, TILE], F32)
        feat_hi = sb("feat_hi", [P, CHUNKS, STEP], F32R)
        feat_lo = sb("feat_lo", [P, CHUNKS, STEP], F32R)
        w1_hi = sb("w1_hi", [P, CHUNKS, H1], F32R)
        w1_lo = sb("w1_lo", [P, CHUNKS, H1], F32R)
        w2_hi = sb("w2_hi", [P, KH1, H2], F32R)
        w2_lo = sb("w2_lo", [P, KH1, H2], F32R)
        w3_sb = sb("w3_sb", [P, KH2], F32)
        b1_sb = sb("b1_sb", [P, KH1], F32)
        b2_sb = sb("b2_sb", [P, KH2], F32)
        h1 = sb("h1", [P, 2, STEP], F32)
        h1_hi = sb("h1_hi", [P, KH1, STEP], F32R)
        h1_lo = sb("h1_lo", [P, KH1, STEP], F32R)
        h2 = sb("h2", [P, KH2, STEP], F32)
        y_sb = sb("y_sb", [1, STEP], F32)

        ps_vec = [psum(f"ps_vec{i}", [P, 512]) for i in range(2)]
        ps_pair = [psum(f"ps_pair{i}", [P, SET_BANKS, 512]) for i in range(2)]
        ps_mlp = [psum(f"ps_mlp{i}", [P, 512]) for i in range(2)]

        stage = vecs[:].rearrange("p t b n -> p (t b n)")
        TAB = ROWS_PER_PART * D
        tab_stage = [stage[0:TABLE_PARTS, i * TAB:(i + 1) * TAB].rearrange("p (r d) -> p r d", d=D)
                     for i in range(NO)]
        w2_stage = stage[:, NO * TAB:NO * TAB + KH1 * H2].rearrange("p (k o) -> p k o", o=H2)
        rows_stage = rows[1][:].rearrange("p g d -> p (g d)")
        C_ROWS = NG * D // H1
        C_VECS = CHUNKS - 1 - C_ROWS
        VECS_AT = NO * TAB + KH1 * H2
        assert VECS_AT + C_VECS * H1 <= TILES * TILE * SLOT
        w1_stage = [(0, C_ROWS, rows_stage[:, 0:C_ROWS * H1].rearrange("p (c h) -> p c h", h=H1)),
                    (C_ROWS, C_VECS, stage[:, VECS_AT:VECS_AT + C_VECS * H1].rearrange("p (c h) -> p c h", h=H1)),
                    (CHUNKS - 1, 1, feat[:].rearrange("p c b -> p (c b)")[:, 0:H1].rearrange("p (c h) -> p c h", h=H1))]

        s_ident = sem("ident_ready")
        s_row_base = sem("row_base_ready")
        s_tab_in = [sem(f"table{i}_landed") for i in range(NO)]
        s_w_in = [sem(f"w1_part{i}_landed") for i in range(3)] + [sem("w2_landed")]
        s_small_in = sem("biases_and_w3_landed")
        s_split_hi = sem("setup_hi_done")
        s_split_lo = sem("setup_lo_done")
        s_pad = sem("pad_slots_zero")
        s_idx = [sem(f"idx{t}_landed") for t in range(TILES)]
        s_dense = [sem(f"dense{t}_landed") for t in range(TILES)]
        s_ids_bc_begun = sem("ids_bc_load_begun")
        s_ids_bc = sem("ids_bc_landed")
        s_row_off = sem("row_off_ready")
        s_tile_begun = sem("tile_gathers_begun")
        s_gathered = [sem(f"rows{t}_gathered") for t in range(TILES)]
        s_onehot = sem("onehot_pieces_ready")
        s_onehot_used = sem("onehot_pieces_used")
        s_vec = sem("transposed_chunks_in_psum")
        s_vec_act = sem("vector_chunks_copied_act")
        s_vec_dve = sem("vector_chunks_copied_dve")
        s_pair = sem("pair_sets_in_psum")
        s_feat_act = sem("pair_sets_copied_act")
        s_feat_dve = sem("pair_sets_copied_dve")
        s_feat_dense = sem("dense_chunk_copied")
        s_feat_hi = sem("feat_hi_ready")
        s_feat_lo = sem("feat_lo_ready")
        s_m1 = sem("mlp1_blocks_in_psum")
        s_h1 = sem("h1_ready")
        s_h1_hi = sem("h1_hi_ready")
        s_h1_lo = sem("h1_lo_ready")
        s_m2 = sem("mlp2_blocks_in_psum")
        s_h2 = sem("h2_ready")
        s_m3 = sem("mlp3_in_psum")
        s_y = sem("y_ready")
        s_out = sem("out_stored")

        N_SPLIT = NO + len(w1_stage) + 1
        splits = ([(s_tab_in[i], tab_stage[i], tab_hi[0:TABLE_PARTS, i], tab_lo[0:TABLE_PARTS, i]) for i in range(NO)]
                  + [(s_w_in[i], st, w1_hi[:, c:c + n], w1_lo[:, c:c + n]) for i, (c, n, st) in enumerate(w1_stage)]
                  + [(s_w_in[3], w2_stage, w2_hi[:], w2_lo[:])])

        def wait_transposed(engine, k, t):
            if not (isinstance(k, int) and k < 0):
                engine.wait_ge(s_vec, k * TILES * T_CHUNKS + (t + 1) * T_CHUNKS)

        def wait_vec_chunk(engine, k, j):
            if j < OH_CHUNKS:
                engine.wait_ge(s_onehot_used, k * PIECES + 4 * (j + 1))
            else:
                engine.wait_ge(s_vec, k * TILES * T_CHUNKS + j - OH_CHUNKS + 1)

        y_dram = out.rearrange("b o -> o b")

        def sample0(k, t):
            return k * STEP + t * TILE

        block = ctx.enter_context(nc.Block())

        @block.sync
        def _(sp):
            def load_idx(k, t):
                wait(sp, s_gathered[t], 16 * NG * k)
                sp.dma_start(idx[t][:], ids[bass.ds(sample0(k, t), TILE), :]).then_inc(s_idx[t], 16)

            def load_dense(k, t):
                wait_transposed(sp, k - 1, t)
                sp.dma_start(dense_in[t][:], dense[bass.ds(sample0(k, t), TILE), :]).then_inc(s_dense[t], 16)

            def load_ids_bc(k):
                wait(sp, s_row_off, k)
                sp.sem_inc(s_ids_bc_begun, 1)
                sp.dma_start(ids_bc[:], ids_onehot[:, bass.ds(k * STEP, STEP)].partition_broadcast(P)).then_inc(s_ids_bc, 16)

            def store_y(k):
                sp.wait_ge(s_y, k + 1)
                sp.dma_start(y_dram[:, bass.ds(k * STEP, STEP)], y_sb[:]).then_inc(s_out, 16)

            load_idx(0, 0)
            load_idx(0, 1)
            load_ids_bc(0)
            for i in range(NO):
                sp.dma_start(tab_stage[i], tables[ONEHOT[i]].rearrange("(p r) d -> p r d", r=ROWS_PER_PART)).then_inc(s_tab_in[i], 16)
            for t in range(TILES):
                load_dense(0, t)

            def loads_for(k):
                load_idx(k, 0)
                load_dense(k, 0)
                load_ids_bc(k)

            loads_for(1)
            load_idx(1, 1)
            load_dense(1, 1)
            with sp.Fori(1, STEPS - 1) as k:
                loads_for(k + 1)
                store_y(k - 1)
                load_idx(k + 1, 1)
                load_dense(k + 1, 1)
            store_y(STEPS - 2)
            store_y(STEPS - 1)
            sp.wait_ge(s_out, 16 * STEPS)

        @block.gpsimd
        def _(pool):
            nc.gpsimd.memset(ident[:], 0.0).then_inc(s_ident, 1)
            pool.wait_ge(s_ident, 1)
            nc.gpsimd.affine_select(out=ident[:], in_=ident[:], compare_op=ALU.not_equal, fill=1.0, base=0,
                                    pattern=[[-1, P]], channel_multiplier=1).then_inc(s_ident, 1)
            nc.gpsimd.iota(row_base[:], pattern=[[0, 1]], base=0, channel_multiplier=ROWS_PER_PART).then_inc(s_row_base, 1)

            def gather(k, t):
                pool.wait_ge(s_idx[t], 16 * (k + 1))
                wait_transposed(pool, k - 1, t)
                pool.sem_inc(s_tile_begun, 1)
                for g, f in enumerate(GATHERED):
                    nc.gpsimd.indirect_dma_start(
                        out=rows[t][:, g, :], out_offset=None, in_=tables[f],
                        in_offset=bass.IndirectOffsetOnAxis(ap=idx[t][:, f:f + 1], axis=0)).then_inc(s_gathered[t], 16)

            gather(0, 0)
            pool.wait_ge(s_split_hi, NO + 1)
            pool.wait_ge(s_split_lo, NO + 1)
            gather(0, 1)
            with pool.Fori(1, STEPS) as k:
                gather(k, 0)
                gather(k, 1)

        @block.tensor
        def _(pe):
            def vec_bank(k, j):
                if j % 2:
                    wait(pe, s_vec_dve, k * V_DVE + j // 2)
                else:
                    wait(pe, s_vec_act, k * V_ACT + j // 2)
                return ps_vec[j % 2]

            def onehot_lookups(k):
                for i in range(NO):
                    if i % 2 == 0:
                        bank = vec_bank(k, i // 2)
                    for half in range(2):
                        q = 2 * i + half
                        pe.wait_ge(s_onehot, k * PIECES + q + 1)
                        for r in range(HALF):
                            row = half * HALF + r
                            for tab in (tab_hi, tab_lo):
                                mm = nc.tensor.matmul(bank[:, (i % 2) * STEP:(i % 2 + 1) * STEP],
                                                      tab[0:TABLE_PARTS, i, row, :], onehot[0:TABLE_PARTS, q % RING, r, :],
                                                      start=(row == 0 and tab is tab_hi),
                                                      stop=(row == ROWS_PER_PART - 1 and tab is tab_lo))
                        mm.then_inc(s_onehot_used, 1)

            def transposes(k, t):
                pe.wait_ge(s_dense[t], 16 * (k + 1))
                pe.wait_ge(s_gathered[t], 16 * NG * (k + 1))
                for c in range(T_CHUNKS):
                    bank = vec_bank(k, OH_CHUNKS + t * T_CHUNKS + c)
                    for v in range(c * PER_CHUNK, min(NT, (c + 1) * PER_CHUNK)):
                        src = dense_in[t][:] if v == 0 else rows[t][:, v - 1, :]
                        at = (v % PER_CHUNK) * TILE
                        mm = nc.tensor.transpose(bank[:, at:at + TILE], src, ident[:])
                    mm.then_inc(s_vec, 1)

            def pair_products(k, t):
                last = OH_CHUNKS + (t + 1) * T_CHUNKS
                pe.wait_ge(s_vec_act, k * V_ACT + (last + 1) // 2)
                pe.wait_ge(s_vec_dve, k * V_DVE + last // 2)
                for u in range(SETS):
                    half = u % 2
                    wait(pe, (s_feat_act, s_feat_dve)[half], k * (TILES * SETS // 2) + t * SETS // 2 + u // 2)
                    for g in range(SET // GROUP):
                        b0 = u * SET + g * GROUP
                        at = (g % BANK_GROUPS) * PRODUCTS
                        mm = nc.tensor.matmul(
                            ps_pair[half][:, g // BANK_GROUPS, at:at + PRODUCTS],
                            vecs[:, t, b0:b0 + GROUP, :].rearrange("p s n -> p (s n)"),
                            vecs[:, t, b0:b0 + GROUP, 0:NVEC], start=True, stop=True)
                    mm.then_inc(s_pair, 1)

            def three_products(acc, w_hi, w_lo, x_hi, x_lo, first, last):
                nc.tensor.matmul(acc, w_hi, x_hi, start=first, stop=False)
                nc.tensor.matmul(acc, w_hi, x_lo, start=False, stop=False)
                return nc.tensor.matmul(acc, w_lo, x_hi, start=False, stop=last)

            def mlp12(k):
                pe.wait_ge(s_feat_hi, TILES * (k + 1))
                pe.wait_ge(s_feat_lo, TILES * (k + 1))
                for f in range(KH1):
                    if f == 0:
                        wait(pe, s_y, k)
                    elif f == 1:
                        wait(pe, s_h2, KH2 * k)
                    else:
                        pe.wait_ge(s_h1_hi, KH1 * k + f - 1)
                    for c in range(CHUNKS):
                        mm = three_products(ps_mlp[f % 2][:, 0:STEP], w1_hi[:, c, f * P:(f + 1) * P],
                                            w1_lo[:, c, f * P:(f + 1) * P], feat_hi[:, c, :], feat_lo[:, c, :],
                                            c == 0, c == CHUNKS - 1)
                    mm.then_inc(s_m1, 1)
                for o, kk in ([(o, kk) for o in range(KH2) for kk in range(KH1 - 1)]
                              + [(o, KH1 - 1) for o in range(KH2)]):
                    if kk == 0:
                        pe.wait_ge(s_h1_hi, KH1 * k + KH1 - 1 + o)
                    pe.wait_ge(s_h1_hi, KH1 * k + kk + 1)
                    pe.wait_ge(s_h1_lo, KH1 * k + kk + 1)
                    mm = three_products(ps_mlp[o][:, 0:STEP], w2_hi[:, kk, o * P:(o + 1) * P],
                                        w2_lo[:, kk, o * P:(o + 1) * P], h1_hi[:, kk, :], h1_lo[:, kk, :],
                                        kk == 0, kk == KH1 - 1)
                    if kk == KH1 - 1:
                        mm.then_inc(s_m2, 1)

            def mlp3(k):
                for kk in range(KH2):
                    pe.wait_ge(s_h2, KH2 * k + kk + 1)
                    mm = nc.tensor.matmul(ps_mlp[0][0:1, 0:STEP], w3_sb[:, kk:kk + 1], h2[:, kk, :],
                                          start=(kk == 0), stop=(kk == KH2 - 1))
                mm.then_inc(s_m3, 1)

            def step(k, first=False):
                onehot_lookups(k)
                transposes(k, 0)
                if not first:
                    mlp12(k - 1)
                transposes(k, 1)
                if not first:
                    mlp3(k - 1)
                pair_products(k, 0)
                pair_products(k, 1)

            pe.wait_ge(s_ident, 2)
            pe.wait_ge(s_split_hi, N_SPLIT)
            pe.wait_ge(s_split_lo, N_SPLIT)
            pe.wait_ge(s_small_in, 48)
            pe.wait_ge(s_pad, 1)
            step(0, first=True)
            with pe.Fori(1, STEPS) as k:
                step(k)
            mlp12(STEPS - 1)
            mlp3(STEPS - 1)

        def vec_dst(j):
            if j < OH_CHUNKS:
                v = NT + 2 * j
                return vecs[:, :, :, v:v + 2].rearrange("p t b n -> p n (t b)"), 2
            t, c = divmod(j - OH_CHUNKS, T_CHUNKS)
            n = min(NT, (c + 1) * PER_CHUNK) - c * PER_CHUNK
            return vecs[:, t, :, c * PER_CHUNK:c * PER_CHUNK + n].rearrange("p b n -> p n b"), n

        def vec_src(j):
            dst, n = vec_dst(j)
            width = STEP if j < OH_CHUNKS else TILE
            return ps_vec[j % 2][:, 0:n * width].rearrange("p (n b) -> p n b", n=n)

        def pair_copies(u, copy):
            src = ps_pair[u % 2][:, :, 0:BANK_GROUPS * PRODUCTS].rearrange("p k (g s m) -> p m k g s", s=GROUP, m=NVEC)
            dst = feat[:, 0:PAIR_COLS, u * SET:(u + 1) * SET].rearrange("p c (k g s) -> p c k g s", k=SET_BANKS, s=GROUP)
            for s in range(GROUP):
                for j in range(BLOCKS):
                    last = copy(dst[SLOT * j:SLOT * (j + 1), :, :, :, s],
                                src[SLOT * s:SLOT * (s + 1), PAIR_START[j]:PAIR_START[j] + PAIR_COLS, :, :, s])
            return last

        @block.scalar
        def _(act):
            for i, (c, n, st) in enumerate(w1_stage):
                act.dma_start(st, w1[:, c:c + n, :]).then_inc(s_w_in[i], 16)
            act.dma_start(w2_stage, w2).then_inc(s_w_in[3], 16)
            act.dma_start(w3_sb[:], w3).then_inc(s_small_in, 16)
            act.dma_start(b1_sb[:], b1).then_inc(s_small_in, 16)
            act.dma_start(b2_sb[:], b2).then_inc(s_small_in, 16)

            for landed, st, hi, _ in splits:
                act.wait_ge(landed, 16)
                nc.scalar.activation(hi, st, ACT.Copy).then_inc(s_split_hi, 1)
            act.wait_ge(s_small_in, 48)

            def vec_copies(k, chunks):
                for j in chunks:
                    if j % 2 == 0:
                        wait_vec_chunk(act, k, j)
                        nc.scalar.activation(vec_dst(j)[0], vec_src(j), ACT.Copy).then_inc(s_vec_act, 1)

            def mlp12(k):
                for f in range(KH1):
                    src = ps_mlp[f % 2][:, 0:STEP]
                    act.wait_ge(s_m1, KH1 * k + f + 1)
                    if f >= 2:
                        act.wait_ge(s_h1_lo, KH1 * k + f - 1)
                    else:
                        wait(act, s_m2, KH2 * k)
                    nc.scalar.activation(h1[:, f % 2, :], src, ACT.Relu, bias=b1_sb[:, f:f + 1]).then_inc(s_h1, 1)
                    nc.scalar.activation(h1_hi[:, f, :], src, ACT.Relu, bias=b1_sb[:, f:f + 1]).then_inc(s_h1_hi, 1)
                for o in range(KH2):
                    act.wait_ge(s_m2, KH2 * k + o + 1)
                    nc.scalar.activation(h2[:, o, :], ps_mlp[o][:, 0:STEP], ACT.Relu, bias=b2_sb[:, o:o + 1]).then_inc(s_h2, 1)

            def mlp3(k):
                act.wait_ge(s_m3, k + 1)
                wait(act, s_out, 16 * k)
                nc.scalar.activation(y_sb[:], ps_mlp[0][0:1, 0:STEP], ACT.Copy).then_inc(s_y, 1)

            def features(k, t):
                wait(act, s_feat_hi, TILES * k + t)
                wait(act, s_feat_lo, TILES * k + t)
                for u in range(0, SETS, 2):
                    act.wait_ge(s_pair, TILES * SETS * k + t * SETS + u + 1)
                    pair_copies(u, lambda dst, src: nc.scalar.activation(dst, src, ACT.Copy)).then_inc(s_feat_act, 1)
                nc.scalar.activation(feat[:, PAIR_COLS, :], vecs[:, t, :, 0], ACT.Copy).then_inc(s_feat_dense, 1)
                act.wait_ge(s_feat_act, (TILES * k + t + 1) * (SETS // 2))
                act.wait_ge(s_feat_dve, (TILES * k + t + 1) * (SETS // 2))
                act.wait_ge(s_feat_dense, TILES * k + t + 1)
                wait(act, s_m1, KH1 * k)
                nc.scalar.activation(feat_hi[:, :, t * TILE:(t + 1) * TILE], feat[:], ACT.Copy).then_inc(s_feat_hi, 1)

            def step(k, first=False):
                vec_copies(k, range(OH_CHUNKS + T_CHUNKS))
                if not first:
                    mlp12(k - 1)
                vec_copies(k, range(OH_CHUNKS + T_CHUNKS, VCHUNKS))
                if not first:
                    mlp3(k - 1)
                features(k, 0)
                features(k, 1)

            step(0, first=True)
            with act.Fori(1, STEPS) as k:
                step(k)
            mlp12(STEPS - 1)
            mlp3(STEPS - 1)

        @block.vector
        def _(dve):
            def row_offsets(k):
                dve.wait_ge(s_ids_bc, 16 * (k + 1))
                wait(dve, s_onehot, PIECES * k)
                nc.vector.tensor_scalar(row_off[:], ids_bc[:], row_base[:], None, ALU.subtract).then_inc(s_row_off, 1)

            def onehot_pieces(k, pieces):
                dve.wait_ge(s_row_off, k + 1)
                for q in pieces:
                    wait(dve, s_onehot_used, PIECES * k + q + 1 - RING)
                    for r in range(HALF):
                        mk = nc.vector.tensor_scalar(onehot[0:TABLE_PARTS, q % RING, r, :],
                                                     row_off[0:TABLE_PARTS, q // 2, :],
                                                     float((q % 2) * HALF + r), None, ALU.is_equal)
                    mk.then_inc(s_onehot, 1)

            def vec_copies(k, chunks):
                for j in chunks:
                    if j % 2:
                        wait_vec_chunk(dve, k, j)
                        nc.vector.tensor_copy(vec_dst(j)[0], vec_src(j)).then_inc(s_vec_dve, 1)

            def mlp12(k):
                for f in range(KH1):
                    dve.wait_ge(s_h1, KH1 * k + f + 1)
                    dve.wait_ge(s_h1_hi, KH1 * k + f + 1)
                    wait(dve, s_m2, KH2 * k)
                    nc.vector.tensor_tensor(h1_lo[:, f, :], h1[:, f % 2, :], h1_hi[:, f, :].bitcast(F32),
                                            ALU.subtract).then_inc(s_h1_lo, 1)

            def feature_sets(k, t, sets):
                for u in sets:
                    dve.wait_ge(s_pair, TILES * SETS * k + t * SETS + u + 1)
                    pair_copies(u, nc.vector.tensor_copy).then_inc(s_feat_dve, 1)

            def feature_low(k, t):
                dve.wait_ge(s_feat_hi, TILES * k + t + 1)
                nc.vector.tensor_tensor(feat_lo[:, :, t * TILE:(t + 1) * TILE], feat[:],
                                        feat_hi[:, :, t * TILE:(t + 1) * TILE].bitcast(F32), ALU.subtract).then_inc(s_feat_lo, 1)

            def step(k, first=False, last=False):
                onehot_pieces(k, range(AHEAD, PIECES - 2))
                vec_copies(k, range(min(2, OH_CHUNKS)))
                onehot_pieces(k, range(PIECES - 2, PIECES))
                vec_copies(k, range(2, OH_CHUNKS + T_CHUNKS))
                if not last:
                    row_offsets(k + 1)
                if not first:
                    mlp12(k - 1)
                vec_copies(k, range(OH_CHUNKS + T_CHUNKS, VCHUNKS))
                for t in range(TILES):
                    wait(dve, s_feat_lo, TILES * k + t)
                    feature_sets(k, t, (1,))
                    if t == TILES - 1 and not last:
                        onehot_pieces(k + 1, range(AHEAD))
                    feature_sets(k, t, range(3, SETS, 2))
                    feature_low(k, t)

            for n, (_, st, hi, lo) in enumerate(splits):
                dve.wait_ge(s_split_hi, n + 1)
                nc.vector.tensor_tensor(lo, st, hi.bitcast(F32), ALU.subtract).then_inc(s_split_lo, 1)
            dve.wait_ge(s_split_lo, N_SPLIT)
            nc.vector.memset(vecs[:, :, :, NVEC:SLOT], 0.0).then_inc(s_pad, 1)
            dve.wait_ge(s_row_base, 1)
            row_offsets(0)
            onehot_pieces(0, range(AHEAD))
            step(0, first=True)
            with dve.Fori(1, STEPS - 1) as k:
                step(k)
            step(STEPS - 1, last=True)
            mlp12(STEPS - 1)


def kernel(**inputs):
    import numpy as np
    import concourse.bacc as bacc
    from concourse.bass_utils import run_bass_kernel_spmd

    nc = bacc.Bacc("TRN2", target_bir_lowering=False, num_devices=1)
    arrays = {}

    def put(name, a):
        a = np.ascontiguousarray(a)
        arrays[name] = a
        return nc.dram_tensor(name, a.shape, mybir.dt.from_np(a.dtype), kind="ExternalInput").ap()

    dense = put("dense", inputs["r_dense"])
    all_ids = np.asarray(inputs["ids"])
    ids = put("ids", all_ids)
    ids_onehot = put("ids_onehot", all_ids.T[list(ONEHOT)])
    tables = [put(f"tbl_{f}", inputs[f"tbl_{f}"]) for f in range(FIELDS)]

    w_top1 = np.asarray(inputs["W_top1"])
    w1 = np.zeros((P, CHUNKS, H1), w_top1.dtype)
    for j, start in enumerate(PAIR_START):
        for c in range(PAIR_COLS):
            m = start + c
            if j and m < PAIR_START[j - 1] + PAIR_COLS:
                continue
            for n in range(m):
                a, b = sorted((VECTORS[n], VECTORS[m]))
                w1[SLOT * j + n, c] = w_top1[a * NVEC - a * (a + 1) // 2 + b - a - 1]
    w1[:, PAIR_COLS] = w_top1[NVEC * (NVEC - 1) // 2:]
    w1 = put("w1", w1)
    b1 = put("b1", np.asarray(inputs["b_top1"]).reshape(H1 // P, P).T)
    w2 = put("w2", np.asarray(inputs["W_top2"]).reshape(H1 // P, P, H2).transpose(1, 0, 2))
    b2 = put("b2", np.asarray(inputs["b_top2"]).reshape(H2 // P, P).T)
    w3 = put("w3", np.asarray(inputs["W_top3"]).reshape(H2 // P, P).T)
    out = nc.dram_tensor("y", (BATCH, 1), F32, kind="ExternalOutput").ap()
    bass_dlrm_tower(nc, dense, ids, ids_onehot, tables, w1, b1, w2, b2, w3, out)
    r = run_bass_kernel_spmd(nc, [arrays], core_ids=[0])
    return r.results[0]["y"]
```

```python
from contextlib import ExitStack

import concourse.bass as bass
from concourse import mybir

F32 = mybir.dt.float32
F32R = mybir.dt.float32r
I32 = mybir.dt.int32
ALU = mybir.AluOpType
ACT = mybir.ActivationFunctionType

P = 128
BATCH, FIELDS, D = 2048, 26, 128
H1, H2 = 512, 256

ONEHOT = (1, 2, 4, 7, 8, 10)
GATHERED = tuple(f for f in range(FIELDS) if f not in ONEHOT)
TABLE_ROWS = 1000
ROWS_PER_PART = 8
TABLE_PARTS = TABLE_ROWS // ROWS_PER_PART

VECTORS = (0,) + tuple(f + 1 for f in GATHERED) + tuple(f + 1 for f in ONEHOT)
NVEC = len(VECTORS)
SLOT = 32

TILE = 128
TILES = 2
STEP = TILE * TILES
STEPS = BATCH // STEP

PAIR_COLS = 7
PAIR_START = (0, 7, 14, NVEC - PAIR_COLS)
BLOCKS = len(PAIR_START)
CHUNKS = PAIR_COLS + 1


def bass_dlrm_tower(nc, dense, ids, ids_onehot, tables, w1, b1, w2, b2, w3, out):
    NG, NO = len(GATHERED), len(ONEHOT)
    KH1, KH2 = H1 // P, H2 // P

    PER_CHUNK = 4
    NT = NG + 1
    OH_CHUNKS = NO // 2
    T_CHUNKS = -(-NT // PER_CHUNK)
    VCHUNKS = OH_CHUNKS + TILES * T_CHUNKS
    V_ACT, V_DVE = (VCHUNKS + 1) // 2, VCHUNKS // 2

    GROUP = 4
    SET_BANKS, BANK_GROUPS = 2, 4
    SET = SET_BANKS * BANK_GROUPS * GROUP
    SETS = TILE // SET
    PRODUCTS = GROUP * NVEC

    HALF = ROWS_PER_PART // 2
    PIECES = 2 * NO
    RING = 4
    AHEAD = 4
    assert PIECES % RING == 0 and AHEAD <= RING

    SECOND_HALF = (("chunk", 0), ("chunk", 1), ("set", 0), ("chunk", 2), ("set", 1), ("chunk", 3),
                   ("chunk", 4), ("set", 2), ("chunk", 5), ("set", 3))
    SECOND_HALF_FIRST = tuple(("set", u) for u in range(SETS)) + tuple(("chunk", c) for c in range(T_CHUNKS))
    assert len(SECOND_HALF) == len(SECOND_HALF_FIRST) == T_CHUNKS + SETS
    LAST_PIECES = 4

    ACT_BLOCKS = 3

    def wait(engine, semaphore, value):
        if not (isinstance(value, int) and value <= 0):
            engine.wait_ge(semaphore, value)

    with ExitStack() as ctx:
        def sb(name, shape, dt):
            return ctx.enter_context(nc.sbuf_tensor(name, shape, dt))

        def psum(name, shape):
            return ctx.enter_context(nc.psum_tensor(name, shape, F32))

        def sem(name):
            return ctx.enter_context(nc.semaphore(name))

        ident = sb("ident", [P, P], F32)
        row_base = sb("row_base", [P, 1], I32)
        idx = [sb(f"idx{t}", [P, FIELDS], I32) for t in range(TILES)]
        ids_bc = sb("ids_bc", [P, NO, STEP], I32)
        row_off = ids_bc[:].bitcast(F32)
        onehot = sb("onehot", [P, RING, HALF, STEP], F32R)
        tab_hi = sb("tab_hi", [P, NO, ROWS_PER_PART, D], F32R)
        tab_lo = sb("tab_lo", [P, NO, ROWS_PER_PART, D], F32R)
        rows = [sb(f"rows{t}", [P, NG, D], F32) for t in range(TILES)]
        dense_in = [sb(f"dense_in{t}", [P, D], F32) for t in range(TILES)]
        vecs = sb("vecs", [P, TILES, TILE, SLOT], F32)
        feat = [sb(f"feat{t}", [P, CHUNKS, TILE], F32) for t in range(TILES)]
        feat_hi = sb("feat_hi", [P, CHUNKS, STEP], F32R)
        feat_lo = sb("feat_lo", [P, CHUNKS, STEP], F32R)
        w1_hi = sb("w1_hi", [P, CHUNKS, H1], F32R)
        w1_lo = sb("w1_lo", [P, CHUNKS, H1], F32R)
        w2_hi = sb("w2_hi", [P, KH1, H2], F32R)
        w2_lo = sb("w2_lo", [P, KH1, H2], F32R)
        w3_sb = sb("w3_sb", [P, KH2], F32)
        b1_sb = sb("b1_sb", [P, KH1], F32)
        b2_sb = sb("b2_sb", [P, KH2], F32)
        h1 = sb("h1", [P, 2, STEP], F32)
        h1_hi = sb("h1_hi", [P, KH1, STEP], F32R)
        h1_lo = sb("h1_lo", [P, KH1, STEP], F32R)
        h2 = sb("h2", [P, KH2, STEP], F32)
        y_sb = sb("y_sb", [1, STEP], F32)

        ps_vec = [psum(f"ps_vec{i}", [P, 512]) for i in range(2)]
        ps_pair = [psum(f"ps_pair{i}", [P, SET_BANKS, 512]) for i in range(2)]
        ps_mlp = [psum(f"ps_mlp{i}", [P, 512]) for i in range(2)]

        stage = vecs[:].rearrange("p t b n -> p (t b n)")
        TAB = ROWS_PER_PART * D
        tab_stage = [stage[0:TABLE_PARTS, i * TAB:(i + 1) * TAB].rearrange("p (r d) -> p r d", d=D)
                     for i in range(NO)]
        w2_stage = stage[:, NO * TAB:NO * TAB + KH1 * H2].rearrange("p (k o) -> p k o", o=H2)
        rows_stage = rows[1][:].rearrange("p g d -> p (g d)")
        C_ROWS = NG * D // H1
        C_VECS = CHUNKS - 1 - C_ROWS
        VECS_AT = NO * TAB + KH1 * H2
        assert VECS_AT + C_VECS * H1 <= TILES * TILE * SLOT
        w1_stage = [(0, C_ROWS, rows_stage[:, 0:C_ROWS * H1].rearrange("p (c h) -> p c h", h=H1)),
                    (C_ROWS, C_VECS, stage[:, VECS_AT:VECS_AT + C_VECS * H1].rearrange("p (c h) -> p c h", h=H1)),
                    (CHUNKS - 1, 1, feat[0][:].rearrange("p c b -> p (c b)")[:, 0:H1].rearrange("p (c h) -> p c h", h=H1))]

        s_ident = sem("ident_ready")
        s_row_base = sem("row_base_ready")
        s_tab_in = [sem(f"table{i}_landed") for i in range(NO)]
        s_w_in = [sem(f"w1_part{i}_landed") for i in range(3)] + [sem("w2_landed")]
        s_small_in = sem("biases_and_w3_landed")
        s_split_hi = sem("setup_hi_done")
        s_split_lo = sem("setup_lo_done")
        s_pad = sem("pad_slots_zero")
        s_idx = [sem(f"idx{t}_landed") for t in range(TILES)]
        s_dense = [sem(f"dense{t}_landed") for t in range(TILES)]
        s_ids_bc_begun = sem("ids_bc_load_begun")
        s_ids_bc = sem("ids_bc_landed")
        s_row_off = sem("row_off_ready")
        s_tile_begun = sem("tile_gathers_begun")
        s_gathered = [sem(f"rows{t}_gathered") for t in range(TILES)]
        s_onehot = sem("onehot_pieces_ready")
        s_onehot_used = sem("onehot_pieces_used")
        s_vec = sem("transposed_chunks_in_psum")
        s_vec_act = sem("vector_chunks_copied_act")
        s_vec_dve = sem("vector_chunks_copied_dve")
        s_pair = sem("pair_sets_in_psum")
        s_feat_act = sem("pair_sets_copied_act")
        s_feat_dve = sem("pair_sets_copied_dve")
        s_feat_dense = sem("dense_chunk_copied")
        s_feat_hi = sem("feat_hi_ready")
        s_feat_lo = sem("feat_lo_ready")
        s_m1 = sem("mlp1_blocks_in_psum")
        s_h1 = sem("h1_ready")
        s_h1_hi = sem("h1_hi_ready")
        s_h1_lo = sem("h1_lo_ready")
        s_m2 = sem("mlp2_blocks_in_psum")
        s_h2 = sem("h2_ready")
        s_m3 = sem("mlp3_in_psum")
        s_y = sem("y_ready")
        s_out = sem("out_stored")

        def table_split(i):
            return s_tab_in[i], tab_stage[i], tab_hi[0:TABLE_PARTS, i], tab_lo[0:TABLE_PARTS, i]

        def w1_split(i):
            c, n, staged = w1_stage[i]
            return s_w_in[i], staged, w1_hi[:, c:c + n], w1_lo[:, c:c + n]

        EARLY = 3
        splits = ([table_split(i) for i in range(EARLY)] + [w1_split(0)]
                  + [table_split(i) for i in range(EARLY, NO)]
                  + [w1_split(1), w1_split(2), (s_w_in[3], w2_stage, w2_hi[:], w2_lo[:])])
        N_SPLIT = len(splits)

        def table_splits_done(i):
            return i + 1 + (i >= EARLY)

        def wait_transposed(engine, k, t):
            if not (isinstance(k, int) and k < 0):
                engine.wait_ge(s_vec, k * TILES * T_CHUNKS + (t + 1) * T_CHUNKS)

        def wait_vec_chunk(engine, k, j):
            if j < OH_CHUNKS:
                engine.wait_ge(s_onehot_used, k * PIECES + 4 * (j + 1))
            else:
                engine.wait_ge(s_vec, k * TILES * T_CHUNKS + j - OH_CHUNKS + 1)

        y_dram = out.rearrange("b o -> o b")

        def sample0(k, t):
            return k * STEP + t * TILE

        block = ctx.enter_context(nc.Block())

        @block.sync
        def _(sp):
            def load_idx(k, t):
                wait(sp, s_gathered[t], 16 * NG * k)
                sp.dma_start(idx[t][:], ids[bass.ds(sample0(k, t), TILE), :]).then_inc(s_idx[t], 16)

            def load_dense(k, t):
                wait_transposed(sp, k - 1, t)
                sp.dma_start(dense_in[t][:], dense[bass.ds(sample0(k, t), TILE), :]).then_inc(s_dense[t], 16)

            def load_ids_bc(k):
                wait(sp, s_onehot, PIECES * k)
                sp.sem_inc(s_ids_bc_begun, 1)
                sp.dma_start(ids_bc[:], ids_onehot[:, bass.ds(k * STEP, STEP)].partition_broadcast(P)).then_inc(s_ids_bc, 16)

            def store_y(k):
                sp.wait_ge(s_y, k + 1)
                sp.dma_start(y_dram[:, bass.ds(k * STEP, STEP)], y_sb[:]).then_inc(s_out, 16)

            def load_table(i):
                sp.dma_start(tab_stage[i], tables[ONEHOT[i]].rearrange("(p r) d -> p r d", r=ROWS_PER_PART)).then_inc(s_tab_in[i], 16)

            def load_w1(i):
                c, n, staged = w1_stage[i]
                sp.dma_start(staged, w1[:, c:c + n, :]).then_inc(s_w_in[i], 16)

            load_idx(0, 0)
            load_ids_bc(0)
            for i in range(EARLY):
                load_table(i)
            load_w1(0)
            load_idx(0, 1)
            for i in range(EARLY, NO):
                load_table(i)
            load_dense(0, 0)
            load_w1(1)
            load_w1(2)
            sp.dma_start(w2_stage, w2).then_inc(s_w_in[3], 16)
            load_dense(0, 1)
            sp.dma_start(w3_sb[:], w3).then_inc(s_small_in, 16)
            sp.dma_start(b1_sb[:], b1).then_inc(s_small_in, 16)
            sp.dma_start(b2_sb[:], b2).then_inc(s_small_in, 16)

            def loads_for(k):
                load_idx(k, 0)
                load_dense(k, 0)
                load_ids_bc(k)

            loads_for(1)
            load_idx(1, 1)
            load_dense(1, 1)
            with sp.Fori(1, STEPS - 1) as k:
                loads_for(k + 1)
                store_y(k - 1)
                load_idx(k + 1, 1)
                load_dense(k + 1, 1)
            store_y(STEPS - 2)
            store_y(STEPS - 1)
            sp.wait_ge(s_out, 16 * STEPS)

        @block.gpsimd
        def _(pool):
            nc.gpsimd.memset(ident[:], 0.0).then_inc(s_ident, 1)
            pool.wait_ge(s_ident, 1)
            nc.gpsimd.affine_select(out=ident[:], in_=ident[:], compare_op=ALU.not_equal, fill=1.0, base=0,
                                    pattern=[[-1, P]], channel_multiplier=1).then_inc(s_ident, 1)
            nc.gpsimd.iota(row_base[:], pattern=[[0, 1]], base=0, channel_multiplier=ROWS_PER_PART).then_inc(s_row_base, 1)

            def gather(k, t):
                pool.wait_ge(s_idx[t], 16 * (k + 1))
                wait_transposed(pool, k - 1, t)
                pool.sem_inc(s_tile_begun, 1)
                for g, f in enumerate(GATHERED):
                    nc.gpsimd.indirect_dma_start(
                        out=rows[t][:, g, :], out_offset=None, in_=tables[f],
                        in_offset=bass.IndirectOffsetOnAxis(ap=idx[t][:, f:f + 1], axis=0)).then_inc(s_gathered[t], 16)

            gather(0, 0)
            pool.wait_ge(s_split_hi, EARLY + 1)
            pool.wait_ge(s_split_lo, EARLY + 1)
            gather(0, 1)
            with pool.Fori(1, STEPS) as k:
                gather(k, 0)
                gather(k, 1)

        @block.tensor
        def _(pe):
            def vec_bank(k, j):
                if j % 2:
                    wait(pe, s_vec_dve, k * V_DVE + j // 2)
                else:
                    wait(pe, s_vec_act, k * V_ACT + j // 2)
                return ps_vec[j % 2]

            def onehot_lookups(k, first):
                for i in range(NO):
                    if first:
                        pe.wait_ge(s_split_hi, table_splits_done(i))
                        pe.wait_ge(s_split_lo, table_splits_done(i))
                    if i % 2 == 0:
                        bank = vec_bank(k, i // 2)
                    for half in range(2):
                        q = 2 * i + half
                        pe.wait_ge(s_onehot, k * PIECES + q + 1)
                        for r in range(HALF):
                            row = half * HALF + r
                            for tab in (tab_hi, tab_lo):
                                mm = nc.tensor.matmul(bank[:, (i % 2) * STEP:(i % 2 + 1) * STEP],
                                                      tab[0:TABLE_PARTS, i, row, :], onehot[0:TABLE_PARTS, q % RING, r, :],
                                                      start=(row == 0 and tab is tab_hi),
                                                      stop=(row == ROWS_PER_PART - 1 and tab is tab_lo))
                        mm.then_inc(s_onehot_used, 1)

            def transpose_chunk(k, t, c):
                if c == 0:
                    pe.wait_ge(s_dense[t], 16 * (k + 1))
                    pe.wait_ge(s_gathered[t], 16 * NG * (k + 1))
                bank = vec_bank(k, OH_CHUNKS + t * T_CHUNKS + c)
                for v in range(c * PER_CHUNK, min(NT, (c + 1) * PER_CHUNK)):
                    src = dense_in[t][:] if v == 0 else rows[t][:, v - 1, :]
                    at = (v % PER_CHUNK) * TILE
                    mm = nc.tensor.transpose(bank[:, at:at + TILE], src, ident[:])
                mm.then_inc(s_vec, 1)

            def pair_set(k, t, u):
                if u == 0:
                    last = OH_CHUNKS + (t + 1) * T_CHUNKS
                    pe.wait_ge(s_vec_act, k * V_ACT + (last + 1) // 2)
                    pe.wait_ge(s_vec_dve, k * V_DVE + last // 2)
                wait(pe, s_feat_act, (k * TILES + t) * SETS + u - 1)
                wait(pe, s_feat_dve, (k * TILES + t) * SETS + u - 1)
                for g in range(SET // GROUP):
                    b0 = u * SET + g * GROUP
                    at = (g % BANK_GROUPS) * PRODUCTS
                    mm = nc.tensor.matmul(
                        ps_pair[u % 2][:, g // BANK_GROUPS, at:at + PRODUCTS],
                        vecs[:, t, b0:b0 + GROUP, :].rearrange("p s n -> p (s n)"),
                        vecs[:, t, b0:b0 + GROUP, 0:NVEC], start=True, stop=True)
                mm.then_inc(s_pair, 1)

            def three_products(acc, w_hi, w_lo, x_hi, x_lo, first, last):
                nc.tensor.matmul(acc, w_hi, x_hi, start=first, stop=False)
                nc.tensor.matmul(acc, w_hi, x_lo, start=False, stop=False)
                return nc.tensor.matmul(acc, w_lo, x_hi, start=False, stop=last)

            def mlp1(k, f, chunks, last=False):
                if f == 0 and 0 in chunks:
                    pe.wait_ge(s_feat_hi, TILES * (k + 1))
                    pe.wait_ge(s_feat_lo, TILES * (k + 1))
                elif f == 0 and last and chunks[0] % (CHUNKS // LAST_PIECES) == 0:
                    pe.wait_ge(s_feat_hi, TILES * (k + 1) + chunks[0] // (CHUNKS // LAST_PIECES))
                    pe.wait_ge(s_feat_lo, TILES * (k + 1) + chunks[0] // (CHUNKS // LAST_PIECES))
                if 0 in chunks:
                    if f == 0:
                        wait(pe, s_y, k)
                    elif f == 1:
                        wait(pe, s_h2, KH2 * k)
                    else:
                        pe.wait_ge(s_h1_hi, KH1 * k + f - 1)
                for c in chunks:
                    mm = three_products(ps_mlp[f % 2][:, 0:STEP], w1_hi[:, c, f * P:(f + 1) * P],
                                        w1_lo[:, c, f * P:(f + 1) * P], feat_hi[:, c, :], feat_lo[:, c, :],
                                        c == 0, c == CHUNKS - 1)
                if CHUNKS - 1 in chunks:
                    mm.then_inc(s_m1, 1)

            def mlp2(k):
                for o, kk in ([(o, kk) for o in range(KH2) for kk in range(KH1 - 1)]
                              + [(o, KH1 - 1) for o in range(KH2)]):
                    if kk == 0:
                        pe.wait_ge(s_h1_hi, KH1 * k + KH1 - 1 + o)
                    pe.wait_ge(s_h1_hi, KH1 * k + kk + 1)
                    pe.wait_ge(s_h1_lo, KH1 * k + kk + 1)
                    mm = three_products(ps_mlp[o][:, 0:STEP], w2_hi[:, kk, o * P:(o + 1) * P],
                                        w2_lo[:, kk, o * P:(o + 1) * P], h1_hi[:, kk, :], h1_lo[:, kk, :],
                                        kk == 0, kk == KH1 - 1)
                    if kk == KH1 - 1:
                        mm.then_inc(s_m2, 1)

            def mlp3(k):
                for kk in range(KH2):
                    pe.wait_ge(s_h2, KH2 * k + kk + 1)
                    mm = nc.tensor.matmul(ps_mlp[0][0:1, 0:STEP], w3_sb[:, kk:kk + 1], h2[:, kk, :],
                                          start=(kk == 0), stop=(kk == KH2 - 1))
                mm.then_inc(s_m3, 1)

            def step(k, first=False):
                onehot_lookups(k, first)
                if first:
                    pe.wait_ge(s_ident, 2)
                for c in range(T_CHUNKS):
                    transpose_chunk(k, 0, c)
                    if not first:
                        mlp1(k - 1, 0, range(CHUNKS)[c * CHUNKS // T_CHUNKS:(c + 1) * CHUNKS // T_CHUNKS])
                if first:
                    pe.wait_ge(s_pad, 1)
                    pe.wait_ge(s_split_hi, N_SPLIT)
                    pe.wait_ge(s_split_lo, N_SPLIT)
                    pe.wait_ge(s_small_in, 48)
                else:
                    for f in range(1, KH1):
                        mlp1(k - 1, f, range(CHUNKS))
                    mlp2(k - 1)
                for kind, n in SECOND_HALF_FIRST if first else SECOND_HALF:
                    if kind == "chunk":
                        transpose_chunk(k, 1, n)
                    else:
                        pair_set(k, 0, n)
                        if n == 0 and not first:
                            mlp3(k - 1)
                for u in range(SETS):
                    pair_set(k, 1, u)

            step(0, first=True)
            with pe.Fori(1, STEPS) as k:
                step(k)
            for c in range(CHUNKS):
                mlp1(STEPS - 1, 0, (c,), last=True)
            for f in range(1, KH1):
                mlp1(STEPS - 1, f, range(CHUNKS))
            mlp2(STEPS - 1)
            mlp3(STEPS - 1)

        def vec_dst(j):
            if j < OH_CHUNKS:
                v = NT + 2 * j
                return vecs[:, :, :, v:v + 2].rearrange("p t b n -> p n (t b)"), 2
            t, c = divmod(j - OH_CHUNKS, T_CHUNKS)
            n = min(NT, (c + 1) * PER_CHUNK) - c * PER_CHUNK
            return vecs[:, t, :, c * PER_CHUNK:c * PER_CHUNK + n].rearrange("p b n -> p n b"), n

        def vec_src(j):
            dst, n = vec_dst(j)
            width = STEP if j < OH_CHUNKS else TILE
            return ps_vec[j % 2][:, 0:n * width].rearrange("p (n b) -> p n b", n=n)

        def pair_copies(t, u, blocks, copy):
            src = ps_pair[u % 2][:, :, 0:BANK_GROUPS * PRODUCTS].rearrange("p k (g s m) -> p m k g s", s=GROUP, m=NVEC)
            dst = feat[t][:, 0:PAIR_COLS, u * SET:(u + 1) * SET].rearrange("p c (k g s) -> p c k g s", k=SET_BANKS, s=GROUP)
            for s in blocks:
                for j in range(BLOCKS):
                    last = copy(dst[SLOT * j:SLOT * (j + 1), :, :, :, s],
                                src[SLOT * s:SLOT * (s + 1), PAIR_START[j]:PAIR_START[j] + PAIR_COLS, :, :, s])
            return last

        @block.scalar
        def _(act):
            for landed, st, hi, _ in splits:
                act.wait_ge(landed, 16)
                nc.scalar.activation(hi, st, ACT.Copy).then_inc(s_split_hi, 1)
            act.wait_ge(s_small_in, 48)
            act.wait_ge(s_split_lo, N_SPLIT)

            def vec_copies(k, chunks):
                for j in chunks:
                    if j % 2 == 0:
                        wait_vec_chunk(act, k, j)
                        nc.scalar.activation(vec_dst(j)[0], vec_src(j), ACT.Copy).then_inc(s_vec_act, 1)

            def mlp12(k):
                for f in range(KH1):
                    src = ps_mlp[f % 2][:, 0:STEP]
                    act.wait_ge(s_m1, KH1 * k + f + 1)
                    if f >= 2:
                        act.wait_ge(s_h1_lo, KH1 * k + f - 1)
                    else:
                        wait(act, s_m2, KH2 * k)
                    nc.scalar.activation(h1[:, f % 2, :], src, ACT.Relu, bias=b1_sb[:, f:f + 1]).then_inc(s_h1, 1)
                    nc.scalar.activation(h1_hi[:, f, :], src, ACT.Relu, bias=b1_sb[:, f:f + 1]).then_inc(s_h1_hi, 1)
                for o in range(KH2):
                    act.wait_ge(s_m2, KH2 * k + o + 1)
                    nc.scalar.activation(h2[:, o, :], ps_mlp[o][:, 0:STEP], ACT.Relu, bias=b2_sb[:, o:o + 1]).then_inc(s_h2, 1)

            def mlp3(k):
                act.wait_ge(s_m3, k + 1)
                wait(act, s_out, 16 * k)
                nc.scalar.activation(y_sb[:], ps_mlp[0][0:1, 0:STEP], ACT.Copy).then_inc(s_y, 1)

            def feature_set(k, t, u):
                if u == 0:
                    wait(act, s_feat_hi, TILES * (k - 1) + t + 1)
                    wait(act, s_feat_lo, TILES * (k - 1) + t + 1)
                act.wait_ge(s_pair, (TILES * k + t) * SETS + u + 1)
                pair_copies(t, u, range(ACT_BLOCKS),
                            lambda dst, src: nc.scalar.activation(dst, src, ACT.Copy)).then_inc(s_feat_act, 1)

            def feature_high(k, t, pieces=1):
                nc.scalar.activation(feat[t][:, PAIR_COLS, :], vecs[:, t, :, 0], ACT.Copy).then_inc(s_feat_dense, 1)
                act.wait_ge(s_feat_act, (TILES * k + t + 1) * SETS)
                act.wait_ge(s_feat_dve, (TILES * k + t + 1) * SETS)
                act.wait_ge(s_feat_dense, TILES * k + t + 1)
                wait(act, s_m1, KH1 * k)
                n = CHUNKS // pieces
                for c in range(0, CHUNKS, n):
                    nc.scalar.activation(feat_hi[:, c:c + n, t * TILE:(t + 1) * TILE], feat[t][:, c:c + n],
                                         ACT.Copy).then_inc(s_feat_hi, 1)

            def step(k, first=False, last=False):
                vec_copies(k, range(OH_CHUNKS + T_CHUNKS))
                if not first:
                    mlp12(k - 1)
                for kind, n in SECOND_HALF_FIRST if first else SECOND_HALF:
                    if kind == "chunk":
                        vec_copies(k, (OH_CHUNKS + T_CHUNKS + n,))
                    else:
                        feature_set(k, 0, n)
                        if n == 0 and not first:
                            mlp3(k - 1)
                for u in range(SETS):
                    feature_set(k, 1, u)
                    if u == 1:
                        feature_high(k, 0)
                feature_high(k, 1, LAST_PIECES if last else 1)

            step(0, first=True)
            with act.Fori(1, STEPS - 1) as k:
                step(k)
            step(STEPS - 1, last=True)
            mlp12(STEPS - 1)
            mlp3(STEPS - 1)

        @block.vector
        def _(dve):
            def row_offsets(k):
                dve.wait_ge(s_ids_bc, 16 * (k + 1))
                nc.vector.tensor_scalar(row_off[:], ids_bc[:], row_base[:], None, ALU.subtract).then_inc(s_row_off, 1)

            def onehot_pieces(k, pieces):
                dve.wait_ge(s_row_off, k + 1)
                for q in pieces:
                    wait(dve, s_onehot_used, PIECES * k + q + 1 - RING)
                    for r in range(HALF):
                        mk = nc.vector.tensor_scalar(onehot[0:TABLE_PARTS, q % RING, r, :],
                                                     row_off[0:TABLE_PARTS, q // 2, :],
                                                     float((q % 2) * HALF + r), None, ALU.is_equal)
                    mk.then_inc(s_onehot, 1)

            def vec_copies(k, chunks):
                for j in chunks:
                    if j % 2:
                        wait_vec_chunk(dve, k, j)
                        nc.vector.tensor_copy(vec_dst(j)[0], vec_src(j)).then_inc(s_vec_dve, 1)

            def mlp12(k):
                for f in range(KH1):
                    dve.wait_ge(s_h1, KH1 * k + f + 1)
                    dve.wait_ge(s_h1_hi, KH1 * k + f + 1)
                    wait(dve, s_m2, KH2 * k)
                    nc.vector.tensor_tensor(h1_lo[:, f, :], h1[:, f % 2, :], h1_hi[:, f, :].bitcast(F32),
                                            ALU.subtract).then_inc(s_h1_lo, 1)

            def feature_set(k, t, u):
                if u == 0:
                    wait(dve, s_feat_lo, TILES * (k - 1) + t + 1)
                dve.wait_ge(s_pair, (TILES * k + t) * SETS + u + 1)
                pair_copies(t, u, range(ACT_BLOCKS, GROUP), nc.vector.tensor_copy).then_inc(s_feat_dve, 1)

            def feature_low(k, t, pieces=1):
                n = CHUNKS // pieces
                for c in range(0, CHUNKS, n):
                    dve.wait_ge(s_feat_hi, TILES * k + t + 1 + c // n)
                    nc.vector.tensor_tensor(feat_lo[:, c:c + n, t * TILE:(t + 1) * TILE], feat[t][:, c:c + n],
                                            feat_hi[:, c:c + n, t * TILE:(t + 1) * TILE].bitcast(F32),
                                            ALU.subtract).then_inc(s_feat_lo, 1)

            def split_low(n):
                dve.wait_ge(s_split_hi, n + 1)
                _, staged, hi, lo = splits[n]
                nc.vector.tensor_tensor(lo, staged, hi.bitcast(F32), ALU.subtract).then_inc(s_split_lo, 1)

            def onehots(k):
                onehot_pieces(k, range(AHEAD, AHEAD + 3))
                feature_low(k - 1, 1)
                onehot_pieces(k, range(AHEAD + 3, PIECES - 2))
                vec_copies(k, range(2))
                onehot_pieces(k, range(PIECES - 2, PIECES))

            def first_onehots():
                for n in range(EARLY + 1):
                    split_low(n)
                onehot_pieces(0, range(AHEAD, AHEAD + 2))
                split_low(EARLY + 1)
                onehot_pieces(0, range(AHEAD + 2, AHEAD + 4))
                for n in range(EARLY + 2, N_SPLIT):
                    split_low(n)
                onehot_pieces(0, range(AHEAD + 4, PIECES - 2))
                dve.wait_ge(s_split_lo, N_SPLIT)
                vec_copies(0, range(2))
                onehot_pieces(0, range(PIECES - 2, PIECES))
                nc.vector.memset(vecs[:, :, :, NVEC:SLOT], 0.0).then_inc(s_pad, 1)

            def step(k, first=False, last=False):
                if first:
                    first_onehots()
                else:
                    onehots(k)
                vec_copies(k, range(2, OH_CHUNKS + T_CHUNKS))
                if not first:
                    mlp12(k - 1)
                if not last:
                    row_offsets(k + 1)
                for kind, n in SECOND_HALF_FIRST if first else SECOND_HALF:
                    if kind == "chunk":
                        vec_copies(k, (OH_CHUNKS + T_CHUNKS + n,))
                    else:
                        feature_set(k, 0, n)
                        if not last:
                            onehot_pieces(k + 1, range(n * AHEAD // SETS, (n + 1) * AHEAD // SETS))
                for u in range(SETS):
                    feature_set(k, 1, u)
                    if u == 2:
                        feature_low(k, 0)

            dve.wait_ge(s_row_base, 1)
            row_offsets(0)
            onehot_pieces(0, range(AHEAD))
            step(0, first=True)
            with dve.Fori(1, STEPS - 1) as k:
                step(k)
            step(STEPS - 1, last=True)
            feature_low(STEPS - 1, 1, LAST_PIECES)
            mlp12(STEPS - 1)


def kernel(**inputs):
    import numpy as np
    import concourse.bacc as bacc
    from concourse.bass_utils import run_bass_kernel_spmd

    nc = bacc.Bacc("TRN2", target_bir_lowering=False, num_devices=1)
    arrays = {}

    def put(name, a):
        a = np.ascontiguousarray(a)
        arrays[name] = a
        return nc.dram_tensor(name, a.shape, mybir.dt.from_np(a.dtype), kind="ExternalInput").ap()

    dense = put("dense", inputs["r_dense"])
    all_ids = np.asarray(inputs["ids"])
    ids = put("ids", all_ids)
    ids_onehot = put("ids_onehot", all_ids.T[list(ONEHOT)])
    tables = [put(f"tbl_{f}", inputs[f"tbl_{f}"]) for f in range(FIELDS)]

    w_top1 = np.asarray(inputs["W_top1"])
    w1 = np.zeros((P, CHUNKS, H1), w_top1.dtype)
    for j, start in enumerate(PAIR_START):
        for c in range(PAIR_COLS):
            m = start + c
            if j and m < PAIR_START[j - 1] + PAIR_COLS:
                continue
            for n in range(m):
                a, b = sorted((VECTORS[n], VECTORS[m]))
                w1[SLOT * j + n, c] = w_top1[a * NVEC - a * (a + 1) // 2 + b - a - 1]
    w1[:, PAIR_COLS] = w_top1[NVEC * (NVEC - 1) // 2:]
    w1 = put("w1", w1)
    b1 = put("b1", np.asarray(inputs["b_top1"]).reshape(H1 // P, P).T)
    w2 = put("w2", np.asarray(inputs["W_top2"]).reshape(H1 // P, P, H2).transpose(1, 0, 2))
    b2 = put("b2", np.asarray(inputs["b_top2"]).reshape(H2 // P, P).T)
    w3 = put("w3", np.asarray(inputs["W_top3"]).reshape(H2 // P, P).T)
    out = nc.dram_tensor("y", (BATCH, 1), F32, kind="ExternalOutput").ap()
    bass_dlrm_tower(nc, dense, ids, ids_onehot, tables, w1, b1, w2, b2, w3, out)
    r = run_bass_kernel_spmd(nc, [arrays], core_ids=[0])
    return r.results[0]["y"]
```

```python
from contextlib import ExitStack

import concourse.bass as bass
import numpy as np
from concourse import mybir

F32 = mybir.dt.float32
F32R = mybir.dt.float32r
I32 = mybir.dt.int32
ALU = mybir.AluOpType
ACT = mybir.ActivationFunctionType

P = 128
BATCH, FIELDS, D = 2048, 26, 128
H1, H2 = 512, 256

ONEHOT = (12, 1, 2, 4, 7, 8, 10, 14)
GATHERED = tuple(f for f in range(FIELDS) if f not in ONEHOT) + ONEHOT[:1]
TABLE_ROWS = 1000
ROWS_PER_PART = 8
TABLE_PARTS = TABLE_ROWS // ROWS_PER_PART

VECTORS = (0,) + tuple(f + 1 for f in GATHERED) + tuple(f + 1 for f in ONEHOT[1:])
NVEC = len(VECTORS)
SLOT = 32

TILE = 128
TILES = 2
STEP = TILE * TILES
STEPS = BATCH // STEP

GROUP_COLS = 3
GROUPS = NVEC // GROUP_COLS
BLOCK_GROUPS = ((0, 1, 2), (3, 4), (5, 6), (7, 8))
FEAT_COLS = GROUP_COLS * max(len(groups) for groups in BLOCK_GROUPS)
GROUP_ROWS = tuple({17: 18, 23: 24}.get(rows, rows) for rows in (GROUP_COLS * (g + 1) - 1 for g in range(GROUPS)))
PACKED_AT = tuple(sum(GROUP_ROWS[:g]) for g in range(GROUPS))
assert sum(GROUP_ROWS) == P
CHUNKS = GROUP_COLS + 1
DENSE_CHUNK = GROUP_COLS


def bass_dlrm_tower(nc, dense, ids, ids_onehot, tables, w1, b1, w2, b2, w3, out):
    NG, NO = len(GATHERED), len(ONEHOT)
    KH1, KH2 = H1 // P, H2 // P

    PER_CHUNK = 4
    NT = NG + 1
    OH_CHUNKS = NO // 2
    assert NO % 2 == 0

    def first_table(full):
        return 0 if full else 1

    T_CHUNKS = -(-NT // PER_CHUNK)
    PART_OF_CHUNK = tuple(c // 2 for c in range(T_CHUNKS))
    PART_OF_ROW = tuple(PART_OF_CHUNK[(g + 1) // PER_CHUNK] for g in range(NG))
    PARTS = PART_OF_CHUNK[-1] + 1

    def n_rows(full):
        return NT - 1 if full else NT

    def rows_before(k, part):
        rows = PART_OF_ROW.count(part)
        return 0 if isinstance(k, int) and k == 0 else rows * k - (part == PARTS - 1)

    FIRST_HALF = (("onehot", 0), ("onehot", 1), ("rows", 0), ("rows", 1), ("onehot", 2),
                  ("rows", 2), ("rows", 3), ("onehot", 3), ("rows", 4))
    FIRST_HALF_FIRST = (("onehot", 0), ("onehot", 1), ("onehot", 2), ("rows", 0), ("onehot", 3),
                        ("rows", 1), ("rows", 2), ("rows", 3), ("rows", 4))
    assert sorted(FIRST_HALF) == sorted(FIRST_HALF_FIRST) == [(kind, c) for kind, n in (("onehot", OH_CHUNKS), ("rows", T_CHUNKS))
                                                              for c in range(n)]
    HALF_COPIES = [sum(c % 2 == e for _, c in FIRST_HALF) for e in range(2)]
    COPIES = [HALF_COPIES[e] + sum(c % 2 == e for c in range(T_CHUNKS)) for e in range(2)]

    GROUP = 4
    SET_BANKS, BANK_GROUPS = 2, 4
    SET = SET_BANKS * BANK_GROUPS * GROUP
    SETS = TILE // SET
    PRODUCTS = GROUP * NVEC

    HALF = ROWS_PER_PART // 2
    PIECES = 2 * (NO - 1)
    FULL_PIECES = 2 * NO
    RING = 7
    AHEAD = 7
    assert PIECES % RING == 0 and AHEAD <= RING

    def pieces_before(k):
        return 0 if isinstance(k, int) and k == 0 else PIECES * k + (FULL_PIECES - PIECES)

    def piece_slot(k, q):
        return (q if isinstance(k, int) and k == 0 else q + FULL_PIECES - PIECES) % RING

    SECOND_HALF = (("mlp1", 0), ("set", 0), ("set", 1), ("set", 2), ("mlp1", 1), ("mlp1", 2), ("mlp1", 3),
                   ("rows", 0), ("rows", 1), ("mlp2", 0), ("rows", 2), ("rows", 3), ("mlp3", 0),
                   ("rows", 4), ("set", 3))
    SECOND_HALF_FIRST = tuple(("set", u) for u in range(SETS)) + tuple(("rows", c) for c in range(T_CHUNKS))
    SECOND_HALF_LAST = (("mlp1", 0), ("set", 0), ("set", 1), ("rows", 0), ("rows", 1), ("set", 2),
                        ("rows", 2), ("rows", 3), ("set", 3), ("rows", 4), ("mlp1", 1))
    PIECES_AFTER_SET = (1, 2, 2, 2)
    assert len(PIECES_AFTER_SET) == SETS and sum(PIECES_AFTER_SET) == AHEAD

    ACT_BLOCKS = 3

    MLP1_ORDER = (DENSE_CHUNK,) + tuple(range(GROUP_COLS))

    def wait(engine, semaphore, value):
        if not (isinstance(value, int) and value <= 0):
            engine.wait_ge(semaphore, value)

    with ExitStack() as ctx:
        def sb(name, shape, dt):
            return ctx.enter_context(nc.sbuf_tensor(name, shape, dt))

        def psum(name, shape):
            return ctx.enter_context(nc.psum_tensor(name, shape, F32))

        def sem(name):
            return ctx.enter_context(nc.semaphore(name))

        def low_part(name, shape):
            offset = -(-nc.sbuf_base // 32) * 32
            raw = nc.alloc_sbuf_tensor_at(name + "_raw", shape, F32, offset=offset)
            low = sb(name, shape, F32R)
            assert nc.sbuf_base == offset + 4 * int(np.prod(shape[1:]))
            return low, raw

        ident = sb("ident", [P, P], F32)
        row_base = sb("row_base", [P, 1], I32)
        idx = [sb(f"idx{t}", [P, FIELDS], I32) for t in range(TILES)]
        ids_bc = sb("ids_bc", [P, NO, STEP], I32)
        row_off = ids_bc[:].bitcast(F32)
        onehot = sb("onehot", [P, RING, HALF, STEP], F32R)
        tab_hi = sb("tab_hi", [P, NO, ROWS_PER_PART, D], F32R)
        tab_lo, tab_raw = low_part("tab_lo", [P, NO, ROWS_PER_PART, D])
        rows = [sb(f"rows{t}", [P, NG, D], F32) for t in range(TILES)]
        dense_in = [sb(f"dense_in{t}", [P, D], F32) for t in range(TILES)]
        vecs = sb("vecs", [P, TILES, TILE, SLOT], F32)
        feat = sb("feat", [P, FEAT_COLS, STEP], F32)
        packed = sb("packed", [P, GROUP_COLS, STEP], F32)
        feat_hi = sb("feat_hi", [P, CHUNKS, STEP], F32R)
        feat_lo = sb("feat_lo", [P, CHUNKS, STEP], F32R)
        w1_hi = sb("w1_hi", [P, CHUNKS, H1], F32R)
        w1_lo, w1_raw = low_part("w1_lo", [P, CHUNKS, H1])
        w2_hi = sb("w2_hi", [P, KH1, H2], F32R)
        w2_lo, w2_raw = low_part("w2_lo", [P, KH1, H2])
        w3_sb = sb("w3_sb", [P, KH2], F32)
        b1_sb = sb("b1_sb", [P, KH1], F32)
        b2_sb = sb("b2_sb", [P, KH2], F32)
        h1 = sb("h1", [P, 2, STEP], F32)
        h1_hi = sb("h1_hi", [P, KH1, STEP], F32R)
        h1_lo = sb("h1_lo", [P, KH1, STEP], F32R)
        assert KH2 == 2
        h2 = h1
        y_sb = h1[0:1, 1, :]

        ps_vec = [psum(f"ps_vec{i}", [P, 512]) for i in range(2)]
        ps_pair = [psum(f"ps_pair{i}", [P, SET_BANKS, 512]) for i in range(2)]
        ps_mlp = [psum(f"ps_mlp{i}", [P, 512]) for i in range(2)]

        W1_PIECES = 4
        W1_CHUNKS = CHUNKS // W1_PIECES

        s_ident = sem("ident_ready")
        s_row_base = sem("row_base_ready")
        s_tab_in = [sem(f"table{i}_landed") for i in range(NO)]
        s_w_in = [sem(f"w1_piece{i}_landed") for i in range(W1_PIECES)] + [sem("w2_landed")]
        s_small_in = sem("biases_and_w3_landed")
        s_split_hi = sem("setup_hi_done")
        s_split_lo = sem("setup_lo_done")
        s_pad = sem("pad_slots_zero")
        s_idx = [sem(f"idx{t}_landed") for t in range(TILES)]
        s_dense = [sem(f"dense{t}_landed") for t in range(TILES)]
        s_load_begun = sem("ids_load_begun")
        s_ids_bc = sem("ids_bc_landed")
        s_row_off = sem("row_off_ready")
        s_tile_begun = sem("tile_gathers_begun")
        s_gathered = [[sem(f"rows{t}_part{part}_gathered") for part in range(PARTS)] for t in range(TILES)]
        s_onehot = sem("onehot_pieces_ready")
        s_onehot_used = sem("onehot_pieces_used")
        s_vec = sem("transposed_chunks_in_psum")
        s_vec_act = sem("vector_chunks_copied_act")
        s_vec_dve = sem("vector_chunks_copied_dve")
        s_pair = sem("pair_sets_in_psum")
        s_feat_act = sem("pair_sets_copied_act")
        s_feat_dve = sem("pair_sets_copied_dve")
        s_packed = sem("products_packed")
        s_packed_pool = sem("last_products_packed_by_gpsimd")
        s_packed_hi = sem("packed_products_hi_ready")
        s_packed_lo = sem("packed_products_lo_ready")
        s_dense_hi = sem("dense_chunk_hi_ready")
        s_dense_lo = sem("dense_chunk_lo_ready")
        s_m1 = sem("mlp1_blocks_in_psum")
        s_h1 = sem("h1_ready")
        s_h1_hi = sem("h1_hi_ready")
        s_h1_lo = sem("h1_lo_ready")
        s_m2 = sem("mlp2_blocks_in_psum")
        s_h2 = sem("h2_ready")
        s_m3 = sem("mlp3_in_psum")
        s_y = sem("y_ready")
        s_out = sem("out_stored")

        splits = [(s_tab_in[i],) + tuple(tab[0:TABLE_PARTS, i] for tab in (tab_raw, tab_hi, tab_lo)) for i in range(NO)]
        splits += [(s_w_in[i],) + tuple(w[:, i * W1_CHUNKS:(i + 1) * W1_CHUNKS] for w in (w1_raw, w1_hi, w1_lo))
                   for i in range(W1_PIECES)]
        splits += [(s_w_in[W1_PIECES], w2_raw[:], w2_hi[:], w2_lo[:])]
        N_SPLIT = len(splits)
        assert W1_PIECES == SETS

        def wait_transposed(engine, k, t):
            if not (isinstance(k, int) and k < 0):
                engine.wait_ge(s_vec, k * TILES * T_CHUNKS + (t + 1) * T_CHUNKS)

        def wait_vec_chunk(engine, k, kind, t, c, full):
            if kind == "onehot":
                engine.wait_ge(s_onehot_used, pieces_before(k) + 2 * (2 * c + 2 - first_table(full)))
            else:
                engine.wait_ge(s_vec, (k * TILES + t) * T_CHUNKS + c + 1)

        def vec_bank(kind, t, c):
            return ps_mlp[(c + T_CHUNKS) % 2] if (kind, t) == ("rows", 0) else ps_vec[c % 2]

        def pack(engine, k, groups=range(GROUPS), done=s_packed):
            engine.wait_ge(s_feat_act, (k + 1) * TILES * SETS)
            engine.wait_ge(s_feat_dve, (k + 1) * TILES * SETS)
            wait(engine, s_packed_hi, k)
            wait(engine, s_packed_lo, k)
            for g in groups:
                j = [g in block for block in BLOCK_GROUPS].index(True)
                c, n = GROUP_COLS * BLOCK_GROUPS[j].index(g), GROUP_ROWS[g]
                engine.dma_start(packed[PACKED_AT[g]:PACKED_AT[g] + n],
                                 feat[SLOT * j:SLOT * j + n, c:c + GROUP_COLS]).then_inc(done, 16)

        POOL_GROUPS = (6, 7, 8)

        y_dram = out.rearrange("b o -> o b")

        def sample0(k, t):
            return k * STEP + t * TILE

        block = ctx.enter_context(nc.Block())

        @block.sync
        def _(sp):
            def load_idx(k, t):
                for part in range(PARTS):
                    wait(sp, s_gathered[t][part], 16 * rows_before(k, part))
                    sp.sem_inc(s_load_begun, 1)
                sp.dma_start(idx[t][:], ids[bass.ds(sample0(k, t), TILE), :]).then_inc(s_idx[t], 16)

            def load_dense(k, t):
                wait_transposed(sp, k - 1, t)
                sp.dma_start(dense_in[t][:], dense[bass.ds(sample0(k, t), TILE), :]).then_inc(s_dense[t], 16)

            def load_ids_bc(k):
                wait(sp, s_onehot, pieces_before(k))
                sp.sem_inc(s_load_begun, 1)
                sp.dma_start(ids_bc[:], ids_onehot[:, bass.ds(k * STEP, STEP)].partition_broadcast(P)).then_inc(s_ids_bc, 16)

            def store_y(k):
                sp.wait_ge(s_y, k + 1)
                sp.dma_start(y_dram[:, bass.ds(k * STEP, STEP)], y_sb).then_inc(s_out, 16)

            def load_table(i):
                sp.dma_start(tab_raw[0:TABLE_PARTS, i],
                             tables[ONEHOT[i]].rearrange("(p r) d -> p r d", r=ROWS_PER_PART)).then_inc(s_tab_in[i], 16)

            load_idx(0, 0)
            load_ids_bc(0)
            for i in range(4):
                load_table(i)
            load_idx(0, 1)
            for i in range(4, NO):
                load_table(i)
            load_dense(0, 0)
            for i in range(W1_PIECES):
                sp.dma_start(w1_raw[:, i * W1_CHUNKS:(i + 1) * W1_CHUNKS],
                             w1[:, i * W1_CHUNKS:(i + 1) * W1_CHUNKS, :]).then_inc(s_w_in[i], 16)
            sp.dma_start(w2_raw[:], w2).then_inc(s_w_in[W1_PIECES], 16)
            load_dense(0, 1)
            sp.dma_start(w3_sb[:], w3).then_inc(s_small_in, 16)
            sp.dma_start(b1_sb[:], b1).then_inc(s_small_in, 16)
            sp.dma_start(b2_sb[:], b2).then_inc(s_small_in, 16)

            def loads_for(k):
                load_idx(k, 0)
                load_ids_bc(k)
                load_dense(k, 0)

            loads_for(1)
            load_idx(1, 1)
            load_dense(1, 1)
            pack(sp, 0)
            with sp.Fori(1, STEPS - 1) as k:
                loads_for(k + 1)
                store_y(k - 1)
                load_idx(k + 1, 1)
                load_dense(k + 1, 1)
                pack(sp, k)
            pack(sp, STEPS - 1, [g for g in range(GROUPS) if g not in POOL_GROUPS])
            store_y(STEPS - 2)
            store_y(STEPS - 1)
            sp.wait_ge(s_out, 16 * STEPS)

        @block.gpsimd
        def _(pool):
            nc.gpsimd.memset(ident[:], 0.0).then_inc(s_ident, 1)
            pool.wait_ge(s_ident, 1)
            nc.gpsimd.affine_select(out=ident[:], in_=ident[:], compare_op=ALU.not_equal, fill=1.0, base=0,
                                    pattern=[[-1, P]], channel_multiplier=1).then_inc(s_ident, 1)
            nc.gpsimd.iota(row_base[:], pattern=[[0, 1]], base=0, channel_multiplier=ROWS_PER_PART).then_inc(s_row_base, 1)

            def gather(k, t, full=False):
                pool.wait_ge(s_idx[t], 16 * (k + 1))
                wait_transposed(pool, k - 1, t)
                pool.sem_inc(s_tile_begun, 1)
                for g, f in enumerate(GATHERED[:NG - 1] if full else GATHERED):
                    nc.gpsimd.indirect_dma_start(
                        out=rows[t][:, g, :], out_offset=None, in_=tables[f],
                        in_offset=bass.IndirectOffsetOnAxis(ap=idx[t][:, f:f + 1], axis=0)).then_inc(s_gathered[t][PART_OF_ROW[g]], 16)

            gather(0, 0, full=True)
            gather(0, 1, full=True)
            with pool.Fori(1, STEPS - 1) as k:
                gather(k, 0)
                gather(k, 1)
            gather(STEPS - 1, 0, full=True)
            gather(STEPS - 1, 1, full=True)
            pack(pool, STEPS - 1, POOL_GROUPS, s_packed_pool)

        @block.tensor
        def _(pe):
            def wait_copied(k, c, n):
                wait(pe, (s_vec_act, s_vec_dve)[c % 2], k * COPIES[c % 2] + n)

            def wait_chunk_copied(k, order, chunk):
                c = chunk[1]
                wait_copied(k, c, sum(d % 2 == c % 2 for _, d in order[:order.index(chunk) + 1]))

            def onehot_chunk(k, c, order, full):
                if c >= 2:
                    wait_chunk_copied(k, order, ("onehot", c - 2))
                else:
                    wait_copied(k, c, 0)
                for i in range(max(2 * c, first_table(full)), 2 * c + 2):
                    if order is FIRST_HALF_FIRST:
                        pe.wait_ge(s_split_hi, i + 1)
                        pe.wait_ge(s_split_lo, i + 1)
                    for half in range(2):
                        q = 2 * (i - first_table(full)) + half
                        pe.wait_ge(s_onehot, pieces_before(k) + q + 1)
                        for r in range(HALF):
                            row = half * HALF + r
                            for tab in (tab_hi, tab_lo):
                                mm = nc.tensor.matmul(ps_vec[c % 2][:, (i % 2) * STEP:(i % 2 + 1) * STEP],
                                                      tab[0:TABLE_PARTS, i, row, :], onehot[0:TABLE_PARTS, piece_slot(k, q), r, :],
                                                      start=(row == 0 and tab is tab_hi),
                                                      stop=(row == ROWS_PER_PART - 1 and tab is tab_lo))
                        mm.then_inc(s_onehot_used, 1)

            def rows_chunk(k, t, c, order, full):
                if c == 0:
                    pe.wait_ge(s_dense[t], 16 * (k + 1))
                part = PART_OF_CHUNK[c]
                if c == PART_OF_CHUNK.index(part):
                    rows_in = rows_before(k, part) + PART_OF_ROW.count(part)
                    pe.wait_ge(s_gathered[t][part], 16 * (rows_in - (full and part == PARTS - 1)))
                if t == 1:
                    wait_copied(k, c, HALF_COPIES[c % 2] + c // 2)
                elif c >= 2:
                    wait_chunk_copied(k, order, ("rows", c - 2))
                bank = vec_bank("rows", t, c)
                for v in range(c * PER_CHUNK, min(n_rows(full), (c + 1) * PER_CHUNK)):
                    src = dense_in[t][:] if v == 0 else rows[t][:, v - 1, :]
                    at = (v % PER_CHUNK) * TILE
                    mm = nc.tensor.transpose(bank[:, at:at + TILE], src, ident[:])
                mm.then_inc(s_vec, 1)

            def pair_set(k, t, u):
                if u == 0:
                    for e in range(2):
                        wait_copied(k, e, COPIES[e] if t else HALF_COPIES[e])
                wait(pe, s_feat_act, (k * TILES + t) * SETS + u - 1)
                wait(pe, s_feat_dve, (k * TILES + t) * SETS + u - 1)
                for g in range(SET // GROUP):
                    b0 = u * SET + g * GROUP
                    at = (g % BANK_GROUPS) * PRODUCTS
                    mm = nc.tensor.matmul(
                        ps_pair[u % 2][:, g // BANK_GROUPS, at:at + PRODUCTS],
                        vecs[:, t, b0:b0 + GROUP, :].rearrange("p s n -> p (s n)"),
                        vecs[:, t, b0:b0 + GROUP, 0:NVEC], start=True, stop=True)
                mm.then_inc(s_pair, 1)

            def three_products(acc, w_hi, w_lo, x_hi, x_lo, first, last):
                nc.tensor.matmul(acc, w_hi, x_hi, start=first, stop=False)
                nc.tensor.matmul(acc, w_hi, x_lo, start=False, stop=False)
                return nc.tensor.matmul(acc, w_lo, x_hi, start=False, stop=last)

            def mlp1(k, f, chunks, copied_step=None):
                for c in chunks:
                    if c == DENSE_CHUNK:
                        pe.wait_ge(s_dense_hi, k + 1)
                        pe.wait_ge(s_dense_lo, k + 1)
                        if isinstance(k, int) and f == 0:
                            pe.wait_ge(s_y, k)
                        elif isinstance(k, int) and f == 1:
                            pe.wait_ge(s_h2, KH2 * k)
                        if f < 2:
                            if copied_step is not None:
                                wait_chunk_copied(copied_step, FIRST_HALF, ("rows", T_CHUNKS - 2 + f))
                        else:
                            pe.wait_ge(s_h1_hi, KH1 * k + f - 1)
                    else:
                        pe.wait_ge(s_packed_hi, k + 1)
                        pe.wait_ge(s_packed_lo, k + 1)
                    mm = three_products(ps_mlp[f % 2][:, 0:STEP], w1_hi[:, c, f * P:(f + 1) * P],
                                        w1_lo[:, c, f * P:(f + 1) * P], feat_hi[:, c, :], feat_lo[:, c, :],
                                        c == MLP1_ORDER[0], c == MLP1_ORDER[-1])
                if MLP1_ORDER[-1] in chunks:
                    mm.then_inc(s_m1, 1)

            def mlp2(k):
                for o, kk in ([(o, kk) for o in range(KH2) for kk in range(KH1 - 1)]
                              + [(o, KH1 - 1) for o in range(KH2)]):
                    if kk == 0:
                        pe.wait_ge(s_h1_hi, KH1 * k + KH1 - 1 + o)
                    pe.wait_ge(s_h1_hi, KH1 * k + kk + 1)
                    pe.wait_ge(s_h1_lo, KH1 * k + kk + 1)
                    mm = three_products(ps_mlp[o][:, 0:STEP], w2_hi[:, kk, o * P:(o + 1) * P],
                                        w2_lo[:, kk, o * P:(o + 1) * P], h1_hi[:, kk, :], h1_lo[:, kk, :],
                                        kk == 0, kk == KH1 - 1)
                    if kk == KH1 - 1:
                        mm.then_inc(s_m2, 1)

            def mlp3(k):
                for kk in range(KH2):
                    pe.wait_ge(s_h2, KH2 * k + kk + 1)
                    mm = nc.tensor.matmul(ps_mlp[0][0:1, 0:STEP], w3_sb[:, kk:kk + 1], h2[:, kk, :],
                                          start=(kk == 0), stop=(kk == KH2 - 1))
                mm.then_inc(s_m3, 1)

            def step(k, first=False, last=False):
                order = FIRST_HALF_FIRST if first else FIRST_HALF
                if first:
                    pe.wait_ge(s_ident, 2)
                    pe.wait_ge(s_pad, 1)
                for kind, c in order:
                    if kind == "onehot":
                        onehot_chunk(k, c, order, first or last)
                    else:
                        rows_chunk(k, 0, c, order, first or last)
                for kind, n in SECOND_HALF_FIRST if first else SECOND_HALF_LAST if last else SECOND_HALF:
                    if kind == "rows":
                        rows_chunk(k, 1, n, order, first or last)
                    elif kind == "set":
                        pair_set(k, 0, n)
                    elif kind == "mlp1":
                        mlp1(k - 1, n, MLP1_ORDER, copied_step=k)
                    elif kind == "mlp2":
                        mlp2(k - 1)
                    else:
                        mlp3(k - 1)
                for u in range(SETS):
                    pair_set(k, 1, u)
                if last:
                    for f in range(2, KH1):
                        mlp1(k - 1, f, MLP1_ORDER)
                    mlp2(k - 1)
                    mlp3(k - 1)

            step(0, first=True)
            pe.wait_ge(s_split_hi, N_SPLIT)
            pe.wait_ge(s_split_lo, N_SPLIT)
            pe.wait_ge(s_small_in, 48)
            with pe.Fori(1, STEPS - 1) as k:
                step(k)
            step(STEPS - 1, last=True)
            for f in (1, 0):
                mlp1(STEPS - 1, f, MLP1_ORDER[:1])
            for f in range(KH1):
                mlp1(STEPS - 1, f, MLP1_ORDER[1:] if f < 2 else MLP1_ORDER)
            mlp2(STEPS - 1)
            mlp3(STEPS - 1)

        def vec_src_dst(kind, t, c, full):
            if kind == "onehot":
                i, end = max(2 * c, first_table(full)), 2 * c + 2
                dst = vecs[:, :, :, NT - 1 + i:NT - 1 + end].rearrange("p t b n -> p n (t b)")
                start, width = i % 2, STEP
            else:
                i, end = c * PER_CHUNK, min(PER_CHUNK * (c + 1), n_rows(full))
                dst = vecs[:, t, :, i:end].rearrange("p b n -> p n b")
                start, width = 0, TILE
            src = vec_bank(kind, t, c)[:, start * width:(start + end - i) * width]
            return src.rearrange("p (n b) -> p n b", n=end - i), dst

        def pair_copies(t, u, blocks, copy):
            src = ps_pair[u % 2][:, :, 0:BANK_GROUPS * PRODUCTS].rearrange("p k (g s m) -> p m k g s", s=GROUP, m=NVEC)
            dst = feat[:, :, t * TILE + u * SET:t * TILE + (u + 1) * SET].rearrange("p c (k g s) -> p c k g s", k=SET_BANKS, s=GROUP)
            for s in blocks:
                for j, groups in enumerate(BLOCK_GROUPS):
                    m, n = GROUP_COLS * groups[0], GROUP_COLS * len(groups)
                    last = copy(dst[SLOT * j:SLOT * (j + 1), 0:n, :, :, s],
                                src[SLOT * s:SLOT * (s + 1), m:m + n, :, :, s])
            return last

        dense_vec = vecs[:, :, :, 0].rearrange("p t b -> p (t b)")

        @block.scalar
        def _(act):
            def split_high(n):
                landed, raw, hi, _ = splits[n]
                act.wait_ge(landed, 16)
                nc.scalar.activation(hi, raw, ACT.Copy).then_inc(s_split_hi, 1)

            def vec_copies(k, chunks, full, t=0):
                for kind, c in chunks:
                    if c % 2 == 0:
                        wait_vec_chunk(act, k, kind, t, c, full)
                        if (kind, c) == ("rows", 0):
                            wait(act, s_dense_lo, k)
                        src, dst = vec_src_dst(kind, t, c, full)
                        nc.scalar.activation(dst, src, ACT.Copy).then_inc(s_vec_act, 1)

            def mlp1(k, f):
                src = ps_mlp[f % 2][:, 0:STEP]
                act.wait_ge(s_m1, KH1 * k + f + 1)
                if f >= 2:
                    act.wait_ge(s_h1_lo, KH1 * k + f - 1)
                nc.scalar.activation(h1[:, f % 2, :], src, ACT.Relu, bias=b1_sb[:, f:f + 1]).then_inc(s_h1, 1)
                nc.scalar.activation(h1_hi[:, f, :], src, ACT.Relu, bias=b1_sb[:, f:f + 1]).then_inc(s_h1_hi, 1)

            def mlp2(k):
                for o in range(KH2):
                    act.wait_ge(s_m2, KH2 * k + o + 1)
                    nc.scalar.activation(h2[:, o, :], ps_mlp[o][:, 0:STEP], ACT.Relu, bias=b2_sb[:, o:o + 1]).then_inc(s_h2, 1)

            def mlp3(k):
                act.wait_ge(s_m3, k + 1)
                nc.scalar.activation(y_sb, ps_mlp[0][0:1, 0:STEP], ACT.Copy).then_inc(s_y, 1)

            def feature_set(k, t, u):
                if t == 0 and u == 0:
                    wait(act, s_packed, 16 * GROUPS * k)
                act.wait_ge(s_pair, (TILES * k + t) * SETS + u + 1)
                pair_copies(t, u, range(ACT_BLOCKS),
                            lambda dst, src: nc.scalar.activation(dst, src, ACT.Copy)).then_inc(s_feat_act, 1)

            def dense_high(k):
                wait(act, s_m1, KH1 * k)
                nc.scalar.activation(feat_hi[:, DENSE_CHUNK, :], dense_vec, ACT.Copy).then_inc(s_dense_hi, 1)

            def packed_high(k, last=False):
                if last:
                    act.wait_ge(s_packed, 16 * (GROUPS * (k + 1) - len(POOL_GROUPS)))
                    act.wait_ge(s_packed_pool, 16 * len(POOL_GROUPS))
                else:
                    act.wait_ge(s_packed, 16 * GROUPS * (k + 1))
                nc.scalar.activation(feat_hi[:, 0:GROUP_COLS, :], packed[:], ACT.Copy).then_inc(s_packed_hi, 1)

            def step(k, first=False, last=False):
                if first:
                    for i in range(NO):
                        split_high(i)
                    vec_copies(k, FIRST_HALF_FIRST[:3], True)
                    for n in range(NO, N_SPLIT):
                        split_high(n)
                    vec_copies(k, FIRST_HALF_FIRST[3:], True)
                else:
                    vec_copies(k, FIRST_HALF[:4], last)
                    packed_high(k - 1)
                    vec_copies(k, FIRST_HALF[4:], last)
                for kind, n in SECOND_HALF_FIRST if first else SECOND_HALF_LAST if last else SECOND_HALF:
                    if kind == "rows":
                        vec_copies(k, (("rows", n),), first or last, t=1)
                    elif kind == "set":
                        feature_set(k, 0, n)
                    elif kind == "mlp1":
                        mlp1(k - 1, n)
                    elif kind == "mlp2":
                        mlp2(k - 1)
                    else:
                        mlp3(k - 1)
                if first:
                    act.wait_ge(s_small_in, 48)
                for u in range(SETS):
                    feature_set(k, 1, u)
                    if u == 1 and not last:
                        dense_high(k)
                if not first:
                    act.wait_ge(s_out, 16 * (k - 1) if last else 16 * k)
                if last:
                    for f in range(2, KH1):
                        mlp1(k - 1, f)
                    dense_high(k)
                    mlp2(k - 1)
                    mlp3(k - 1)

            step(0, first=True)
            with act.Fori(1, STEPS - 1) as k:
                step(k)
            step(STEPS - 1, last=True)
            packed_high(STEPS - 1, last=True)
            mlp1(STEPS - 1, 0)
            act.wait_ge(s_out, 16 * (STEPS - 1))
            for f in range(1, KH1):
                mlp1(STEPS - 1, f)
            mlp2(STEPS - 1)
            mlp3(STEPS - 1)

        @block.vector
        def _(dve):
            def row_offsets(k):
                dve.wait_ge(s_ids_bc, 16 * (k + 1))
                nc.vector.tensor_scalar(row_off[:], ids_bc[:], row_base[:], None, ALU.subtract).then_inc(s_row_off, 1)

            def onehot_pieces(k, pieces, full=False):
                dve.wait_ge(s_row_off, k + 1)
                for q in pieces:
                    wait(dve, s_onehot_used, pieces_before(k) + q + 1 - RING)
                    for r in range(HALF):
                        mk = nc.vector.tensor_scalar(onehot[0:TABLE_PARTS, piece_slot(k, q), r, :],
                                                     row_off[0:TABLE_PARTS, first_table(full) + q // 2, :],
                                                     float((q % 2) * HALF + r), None, ALU.is_equal)
                    mk.then_inc(s_onehot, 1)

            def vec_copies(k, chunks, full, t=0):
                for kind, c in chunks:
                    if c % 2:
                        wait_vec_chunk(dve, k, kind, t, c, full)
                        src, dst = vec_src_dst(kind, t, c, full)
                        nc.vector.tensor_copy(dst, src).then_inc(s_vec_dve, 1)

            def mlp1(k, f):
                dve.wait_ge(s_h1, KH1 * k + f + 1)
                dve.wait_ge(s_h1_hi, KH1 * k + f + 1)
                nc.vector.tensor_tensor(h1_lo[:, f, :], h1[:, f % 2, :], h1_hi[:, f, :].bitcast(F32),
                                        ALU.subtract).then_inc(s_h1_lo, 1)

            def feature_set(k, t, u):
                if t == 0 and u == 0:
                    wait(dve, s_packed, 16 * GROUPS * k)
                dve.wait_ge(s_pair, (TILES * k + t) * SETS + u + 1)
                pair_copies(t, u, range(ACT_BLOCKS, GROUP), nc.vector.tensor_copy).then_inc(s_feat_dve, 1)

            def dense_low(k):
                dve.wait_ge(s_dense_hi, k + 1)
                nc.vector.tensor_tensor(feat_lo[:, DENSE_CHUNK, :], dense_vec, feat_hi[:, DENSE_CHUNK, :].bitcast(F32),
                                        ALU.subtract).then_inc(s_dense_lo, 1)

            def packed_low(k):
                dve.wait_ge(s_packed_hi, k + 1)
                nc.vector.tensor_tensor(feat_lo[:, 0:GROUP_COLS, :], packed[:], feat_hi[:, 0:GROUP_COLS, :].bitcast(F32),
                                        ALU.subtract).then_inc(s_packed_lo, 1)

            def split_low(n):
                dve.wait_ge(s_split_hi, n + 1)
                _, raw, hi, lo = splits[n]
                nc.vector.tensor_tensor(lo, raw, hi.bitcast(F32), ALU.subtract).then_inc(s_split_lo, 1)

            def first_onehots():
                onehot_pieces(0, range(2), True)
                for i in range(NO):
                    split_low(i)
                    if i < NO - 1:
                        onehot_pieces(0, range(2 * i + 2, 2 * i + 4), True)
                    if i == NO - 3:
                        vec_copies(0, FIRST_HALF_FIRST[:2], True)

            def pieces_after(u):
                return range(sum(PIECES_AFTER_SET[:u]), sum(PIECES_AFTER_SET[:u + 1]))

            def step(k, first=False, before_last=False, last=False):
                if first:
                    first_onehots()
                    vec_copies(k, FIRST_HALF_FIRST[2:], True)
                else:
                    onehot_pieces(k, range(AHEAD, AHEAD + 5), last)
                    vec_copies(k, FIRST_HALF[:4], last)
                    onehot_pieces(k, range(AHEAD + 5, FULL_PIECES if last else PIECES), last)
                    packed_low(k - 1)
                    vec_copies(k, FIRST_HALF[4:], last)
                if not last:
                    row_offsets(k + 1)
                for kind, n in SECOND_HALF_FIRST if first else SECOND_HALF_LAST if last else SECOND_HALF:
                    if kind == "rows":
                        vec_copies(k, (("rows", n),), first or last, t=1)
                    elif kind == "set":
                        feature_set(k, 0, n)
                        if first:
                            split_low(NO + n)
                        elif not last:
                            onehot_pieces(k + 1, pieces_after(n), before_last)
                    elif kind == "mlp1":
                        mlp1(k - 1, n)
                if first:
                    split_low(N_SPLIT - 1)
                for u in range(SETS):
                    feature_set(k, 1, u)
                    if first:
                        onehot_pieces(k + 1, pieces_after(u))
                    if u == 1 and not last:
                        dense_low(k)
                if last:
                    for f in range(2, KH1):
                        mlp1(k - 1, f)
                    dense_low(k)

            nc.vector.memset(vecs[:, :, :, NVEC:SLOT], 0.0).then_inc(s_pad, 1)
            dve.wait_ge(s_row_base, 1)
            row_offsets(0)
            step(0, first=True)
            with dve.Fori(1, STEPS - 2) as k:
                step(k)
            step(STEPS - 2, before_last=True)
            step(STEPS - 1, last=True)
            packed_low(STEPS - 1)
            for f in range(KH1):
                mlp1(STEPS - 1, f)


def kernel(**inputs):
    import numpy as np
    import concourse.bacc as bacc
    from concourse.bass_utils import run_bass_kernel_spmd

    nc = bacc.Bacc("TRN2", target_bir_lowering=False, num_devices=1)
    arrays = {}

    def put(name, a):
        a = np.ascontiguousarray(a)
        arrays[name] = a
        return nc.dram_tensor(name, a.shape, mybir.dt.from_np(a.dtype), kind="ExternalInput").ap()

    dense = put("dense", inputs["r_dense"])
    all_ids = np.asarray(inputs["ids"])
    ids = put("ids", all_ids)
    ids_onehot = put("ids_onehot", all_ids.T[list(ONEHOT)])
    tables = [put(f"tbl_{f}", inputs[f"tbl_{f}"]) for f in range(FIELDS)]

    w_top1 = np.asarray(inputs["W_top1"])
    w1 = np.zeros((P, CHUNKS, H1), w_top1.dtype)
    for g in range(GROUPS):
        for c in range(GROUP_COLS):
            m = GROUP_COLS * g + c
            for n in range(m):
                a, b = sorted((VECTORS[n], VECTORS[m]))
                w1[PACKED_AT[g] + n, c] = w_top1[a * NVEC - a * (a + 1) // 2 + b - a - 1]
    w1[:, DENSE_CHUNK] = w_top1[NVEC * (NVEC - 1) // 2:]
    w1 = put("w1", w1)
    b1 = put("b1", np.asarray(inputs["b_top1"]).reshape(H1 // P, P).T)
    w2 = put("w2", np.asarray(inputs["W_top2"]).reshape(H1 // P, P, H2).transpose(1, 0, 2))
    b2 = put("b2", np.asarray(inputs["b_top2"]).reshape(H2 // P, P).T)
    w3 = put("w3", np.asarray(inputs["W_top3"]).reshape(H2 // P, P).T)
    out = nc.dram_tensor("y", (BATCH, 1), F32, kind="ExternalOutput").ap()
    bass_dlrm_tower(nc, dense, ids, ids_onehot, tables, w1, b1, w2, b2, w3, out)
    r = run_bass_kernel_spmd(nc, [arrays], core_ids=[0])
    return r.results[0]["y"]
```
